# Optimizing a Trainium2 kernel written in Bass

```python
import numpy as np
import jax
import jax.numpy as jnp

def _softmax(x, axis=-1):
    return jax.nn.softmax(x, axis=axis)

def _gelu(x):
    return jax.nn.gelu(x, approximate=True)

def _silu(x):
    return jax.nn.silu(x)

def _sigmoid(x):
    return jax.nn.sigmoid(x)

def _layernorm(x, axis=-1, eps=1e-05):
    m = jnp.mean(x, axis=axis, keepdims=True)
    v = jnp.var(x, axis=axis, keepdims=True)
    return (x - m) / jnp.sqrt(v + eps)

def _scatter_add(tgt, idx, src, axis=0):
    return tgt.at[idx].add(src)

def _segment_sum(src, seg, n):
    return jax.ops.segment_sum(src, seg, n)
kernel_name = 'mk_recurrent_d1_jaxref_r4_81d2bf'

def setup_inputs(seed: int=0):
    np.random.seed(seed)
    _w = jnp.asarray

    def _L0_attn_setup():
        import jax, jax.numpy as jnp
        import numpy as np
        D_MODEL = 256
        NUM_HEADS = 16
        HEAD_DIM = D_MODEL // NUM_HEADS
        MAX_SEQ_LEN = 512

        def _rope_tables(seq_len, head_dim):
            inv_freq = 1.0 / 10000.0 ** (jnp.arange(0, head_dim, 2, dtype=jnp.float32) / head_dim)
            pos = jnp.arange(seq_len, dtype=jnp.float32)
            freqs = jnp.einsum('i,j->ij', pos, inv_freq)
            return (jnp.cos(freqs), jnp.sin(freqs))

        def _apply_rope(x, cos_half, sin_half):
            x_even = x[..., ::2]
            x_odd = x[..., 1::2]
            rot_even = x_even * cos_half - x_odd * sin_half
            rot_odd = x_even * sin_half + x_odd * cos_half
            return jnp.stack([rot_even, rot_odd], axis=-1).reshape(x.shape)
        key = jax.random.key(seed)
        ks = jax.random.split(key, 9)
        B, S = (2, 512)
        glorot = lambda k: jax.random.normal(k, (D_MODEL, D_MODEL), dtype=jnp.float32) * (1.0 / np.sqrt(D_MODEL))
        return {'x': jax.random.normal(ks[0], (B, S, D_MODEL), dtype=jnp.float32), 'wq': glorot(ks[1]), 'bq': jnp.zeros((D_MODEL,), jnp.float32), 'wk': glorot(ks[2]), 'bk': jnp.zeros((D_MODEL,), jnp.float32), 'wv': glorot(ks[3]), 'bv': jnp.zeros((D_MODEL,), jnp.float32), 'wo': glorot(ks[4]), 'bo': jnp.zeros((D_MODEL,), jnp.float32)}
    _L0_attn_in = _L0_attn_setup()

    def _L0_ffn_setup():
        import jax, jax.numpy as jnp
        import numpy as np
        DIM = 256
        HIDDEN = 768
        SCALE = 1.0 / 127.0

        def _dequant(w_int, dtype):
            return w_int.astype(dtype) * jnp.asarray(SCALE, dtype)
        key = jax.random.key(seed)
        k_x, k_g, k_u, k_d = jax.random.split(key, 4)
        x = jax.random.normal(k_x, (4, 512, DIM), dtype=jnp.float32)
        w_gate = jax.random.randint(k_g, (HIDDEN, DIM), -127, 128, dtype=jnp.int32)
        w_up = jax.random.randint(k_u, (HIDDEN, DIM), -127, 128, dtype=jnp.int32)
        w_down = jax.random.randint(k_d, (DIM, HIDDEN), -127, 128, dtype=jnp.int32)
        return {'x': x, 'w_gate': w_gate, 'w_up': w_up, 'w_down': w_down}
    _L0_ffn_in = _L0_ffn_setup()
    _d = {'L0_attn_x': _L0_attn_in['x'], 'L0_attn_wq': _L0_attn_in['wq'], 'L0_attn_bq': _L0_attn_in['bq'], 'L0_attn_wk': _L0_attn_in['wk'], 'L0_attn_bk': _L0_attn_in['bk'], 'L0_attn_wv': _L0_attn_in['wv'], 'L0_attn_bv': _L0_attn_in['bv'], 'L0_attn_wo': _L0_attn_in['wo'], 'L0_attn_bo': _L0_attn_in['bo'], 'L0_ffn_w_gate': _L0_ffn_in['w_gate'], 'L0_ffn_w_up': _L0_ffn_in['w_up'], 'L0_ffn_w_down': _L0_ffn_in['w_down']}
    _x0 = _d['L0_attn_x']
    _d['L0_attn_x'] = jax.random.normal(jax.random.fold_in(jax.random.key(seed), 1), (8, 512, 256), dtype=_x0.dtype)
    del _x0
    return _d

def reference(L0_attn_x, L0_attn_wq, L0_attn_bq, L0_attn_wk, L0_attn_bk, L0_attn_wv, L0_attn_bv, L0_attn_wo, L0_attn_bo, L0_ffn_w_gate, L0_ffn_w_up, L0_ffn_w_down):

    def _L0_attn_ref(x, wq, bq, wk, bk, wv, bv, wo, bo):
        import jax, jax.numpy as jnp
        import numpy as np
        D_MODEL = 256
        NUM_HEADS = 16
        HEAD_DIM = D_MODEL // NUM_HEADS
        MAX_SEQ_LEN = 512

        def _rope_tables(seq_len, head_dim):
            inv_freq = 1.0 / 10000.0 ** (jnp.arange(0, head_dim, 2, dtype=jnp.float32) / head_dim)
            pos = jnp.arange(seq_len, dtype=jnp.float32)
            freqs = jnp.einsum('i,j->ij', pos, inv_freq)
            return (jnp.cos(freqs), jnp.sin(freqs))

        def _apply_rope(x, cos_half, sin_half):
            x_even = x[..., ::2]
            x_odd = x[..., 1::2]
            rot_even = x_even * cos_half - x_odd * sin_half
            rot_odd = x_even * sin_half + x_odd * cos_half
            return jnp.stack([rot_even, rot_odd], axis=-1).reshape(x.shape)
        B, S, _ = x.shape
        q = (x @ wq + bq).reshape(B, S, NUM_HEADS, HEAD_DIM)
        k = (x @ wk + bk).reshape(B, S, NUM_HEADS, HEAD_DIM)
        v = (x @ wv + bv).reshape(B, S, NUM_HEADS, HEAD_DIM)
        cos, sin = _rope_tables(S, HEAD_DIM)
        cos = cos[None, :, None, :]
        sin = sin[None, :, None, :]
        q = _apply_rope(q, cos, sin)
        k = _apply_rope(k, cos, sin)
        q = q.transpose(0, 2, 1, 3)
        k = k.transpose(0, 2, 1, 3)
        v = v.transpose(0, 2, 1, 3)
        scores = jnp.einsum('bhqd,bhkd->bhqk', q, k) / jnp.sqrt(jnp.float32(HEAD_DIM))
        causal = jnp.where(jnp.tril(jnp.ones((S, S), jnp.float32)) == 0, -1000000000.0, 0.0)
        scores = scores + causal
        attn = jax.nn.softmax(scores, axis=-1)
        out = jnp.einsum('bhqk,bhkd->bhqd', attn, v)
        out = out.transpose(0, 2, 1, 3).reshape(B, S, D_MODEL)
        return out @ wo + bo

    def _L0_ffn_ref(x, w_gate, w_up, w_down):
        import jax, jax.numpy as jnp
        import numpy as np
        DIM = 256
        HIDDEN = 768
        SCALE = 1.0 / 127.0

        def _dequant(w_int, dtype):
            return w_int.astype(dtype) * jnp.asarray(SCALE, dtype)
        wg = _dequant(w_gate, x.dtype)
        wu = _dequant(w_up, x.dtype)
        wd = _dequant(w_down, x.dtype)
        gate = jnp.einsum('bsd,hd->bsh', x, wg)
        up = jnp.einsum('bsd,hd->bsh', x, wu)
        h = jax.nn.silu(gate) * up
        return jnp.einsum('bsh,dh->bsd', h, wd)
    x = L0_attn_x
    xn = _layernorm(x, axis=-1)
    s = _L0_attn_ref(xn, L0_attn_wq, L0_attn_bq, L0_attn_wk, L0_attn_bk, L0_attn_wv, L0_attn_bv, L0_attn_wo, L0_attn_bo)
    g = _silu(_L0_ffn_ref(xn, L0_ffn_w_gate, L0_ffn_w_up, L0_ffn_w_down))
    x = x + s * g
    return x

_drawn_inputs = setup_inputs


def setup_inputs(seed=0):
    import zlib

    import numpy as np

    out = dict(_drawn_inputs(seed))
    spreads = {'L0_attn_bq': (0.0, 0.1),
     'L0_attn_bk': (0.0, 0.1),
     'L0_attn_bv': (0.0, 0.1),
     'L0_attn_bo': (0.0, 0.1)}
    factors = {}
    for name, (base, spread) in spreads.items():
        noise = np.random.default_rng([zlib.crc32(name.encode()), seed]).standard_normal(out[name].shape)
        drawn = base * np.exp(spread * noise) if base else spread * noise
        out[name] = jnp.asarray(drawn.astype(out[name].dtype))
    for name, factor in factors.items():
        out[name] = (out[name] * factor).astype(out[name].dtype)
    return out
```

```python
from contextlib import ExitStack

import numpy as np

import concourse.bass as bass
from concourse import mybir

ALU = mybir.AluOpType
ACT = mybir.ActivationFunctionType
AX = mybir.AxisListType
F32 = mybir.dt.float32
F32R = mybir.dt.float32r
I32 = mybir.dt.int32
BF16 = mybir.dt.bfloat16

P = 128
BATCH, SEQ, DM = 8, 512, 256
HEADS, HD = 16, 16
HID = 768
TT = SEQ // P
KT = DM // P
HT = HID // P
PAIRS = HEADS // 2
GROUPS = HEADS // 4
ST = 4 * HD
VW = HD + 1
CHUNKS = 6
SLOTS = 5
WORK_BANKS, B_BANKS = 2, 3
QSCALE = float(HD) ** -0.5
WSCALE = 1.0 / 127.0
EPS = 1e-5
NEG = -1e9 / QSCALE

C_ID, C_MASK, C_COS, C_SIN = 0, P, P + SEQ, P + SEQ + TT * HD
C_ALL = C_SIN + TT * HD


def shape_constants():
    inv_freq = (np.float32(1.0) / np.float32(10000.0) ** (np.arange(0, HD, 2, dtype=np.float32) / np.float32(HD)))
    freqs = np.arange(SEQ, dtype=np.float32)[:, None] * inv_freq.astype(np.float32)[None, :]
    cos, sin = np.cos(freqs), np.sin(freqs)
    cos2 = np.repeat(cos, 2, axis=1)
    sin2 = np.stack([-sin, sin], axis=-1).reshape(SEQ, HD)
    by_tile = lambda t: t.reshape(TT, P, HD).transpose(1, 0, 2).reshape(P, TT * HD)
    mask = np.zeros((P, SEQ), np.float32)
    mask[:, SEQ - P:] = np.where(np.arange(P)[None, :] > np.arange(P)[:, None], NEG, 0.0)
    return np.concatenate([np.eye(P, dtype=np.float32), mask, by_tile(cos2), by_tile(sin2)], axis=1).astype(np.float32)


B_PARTS = [[(h, kt, col) for kt, col in part] for part in ([(0, 0)], [(1, 0), (3, 384)], [(2, 0)]) for h in range(2)]
A_PARTS = [[(h, TT - 1 - kt, col) for h, kt, col in part] for part in B_PARTS]
WIDTH = [SEQ, SEQ, SEQ, SEQ, SEQ // 2, SEQ // 2]


def slot_of(c):
    return (c, 0) if c < 4 else (4, (c - 4) * (SEQ // 2))


P_AT = [[next((slot_of(c)[0], slot_of(c)[1] + col) for c, parts in enumerate(B_PARTS) for hh, k, col in parts
              if (hh, k) == (h, kt)) for h in range(2)] for kt in range(TT)]
PV_ORDER = [0, 1, 3, 2]

WORK = {"T2": ("act", "q_st2_ready"), "T1q": ("act", "q_st_ready"), "T1k": ("act", "k_st_ready"),
        "XT": ("act", "xt_ready"), "QK": ("dve", "qk_ready"), "V": ("dve", "v_ready"), "ON": ("dve", "attn_ready"),
        "AT": ("act", "at_ready"), "OP": ("dve", "prod_ready"), "FT": ("dve", "res_ready"), "G": ("act", "gated"),
        "U": ("dve", "hid_ready"), "DN": ("act", "silu_ready"), "WT": ("act", "wt_ready")}
WT_USES = 11


AHEAD = {"B": 0, "T2": 1, "A": 2, "MX": 2, "T1q": 3, "T1k": 3, "HI": 4, "LO": 4}
STEP = ("PV2 B0 A0 + B1 T1q A1 + PV3 B2 A2 + HI B3 A3 + T1k PV0 B4 + A4 B5 T2 + LO A5 PV1 + MX").split()
STEP_PARTS = STEP.count("+")


def fillers(b, s):
    nb, pb = b + 1, b - 1
    ffn = lambda j: [("G", nb, j), ("U", nb, j)] + ([("HL", nb, j - 1)] if j else [])
    token_tile = lambda t: [("QK", nb, t), ("V", nb, t)] + [("ROPE", nb, 4 * t + k) for k in range(4)]
    return {
        0: [("LN", nb, 0), ("DN", b, 1), ("XT", nb, 0), ("XT", nb, 1)],
        1: token_tile(0) + [("ON", pb, 3)] + token_tile(1),
        2: [("AT", pb, 0), ("AT", pb, 1)] + token_tile(2),
        3: token_tile(3) + [("OP", pb, 0), ("OP", pb, 1), ("ON", b, 0)],
        4: [("FT", pb, 0), ("FT", pb, 1)] + ffn(0),
        5: [("ON", b, 1)] + ffn(1) + ffn(2),
        6: ffn(3) + ffn(4),
        7: [("ON", b, 2)] + ffn(5) + [("HL", nb, 5), ("DN", nb, 0)],
    }[s]


def steps(b):
    items = []
    for s in range(PAIRS):
        fill, at, plus = fillers(b, s), 0, 0
        for token in STEP:
            kind, c = (token[:-1], int(token[-1])) if token[0] in "ABP" else (token, None)
            if kind == "+":
                plus += 1
                upto = len(fill) * plus // STEP_PARTS
                items += fill[at:upto]
                at = upto
            elif kind == "PV":
                if (c < 2) == (s % 2 == 1):
                    g = (b * PAIRS + s - 1) // 2
                    items.append((kind, g // GROUPS, g % GROUPS * TT + c))
            else:
                n = b * PAIRS + s + AHEAD[kind]
                items.append((kind, n // PAIRS, n % PAIRS * (1 if c is None else CHUNKS) + (c or 0)))
    return items


def plan(b):
    items = [item for item in steps(b) if 0 <= item[1] < BATCH]
    if b < 0:
        at = items.index(("G", 0, 0))
        items = [("WQ", 0, 0)] + items[:at] + [("WT", 0, i) for i in range(WT_USES)] + [("FLAG", 0, 0)] + items[at:]
    return items


def epilogue_plan():
    b = BATCH - 1
    return [("PV", b, 14), ("PV", b, 15), ("ON", b, 3), ("AT", b, 0), ("AT", b, 1), ("OP", b, 0), ("OP", b, 1),
            ("FT", b, 0), ("FT", b, 1)]


class Bank:

    def __init__(self):
        self.of, full, kinds, seen = {}, {"act": 0, "dve": 0}, {}, {}
        for b in range(-1, BATCH + 1):
            segment = plan(b) if b < BATCH else epilogue_plan()
            places = [i for i in (steps(b) if 0 <= b < BATCH else segment) if i[0] in WORK]
            for item in segment:
                if item[0] in WORK:
                    kind, first = item[0], WORK[item[0]][0]
                    at = places.index(item) % WORK_BANKS
                    full[first] += 1
                    kinds[kind] = kinds.get(kind, 0) + 1
                    self.of[item] = (at, full[first], seen.get(at))
                    seen[at] = (kind, kinds[kind])
        middle = [i[0] for i in plan(2) if i[0] in WORK]
        self.full_per = {e: sum(WORK[k][0] == e for k in middle) for e in full}
        self.kind_per = {k: middle.count(k) for k in WORK}
        for one, two in zip(plan(1) + plan(2), plan(3) + plan(4)):
            if one[0] in WORK:
                a, b = self.of[one], self.of[two]
                assert a[0] == b[0] and b[1] - a[1] == 2 * self.full_per[WORK[one[0]][0]]
                assert a[2][0] == b[2][0] and b[2][1] - a[2][1] == 2 * self.kind_per[a[2][0]]


def build(nc, x, wq, bq, wk, bk, wv, bv, wo, bo, w_gate, w_up, w_down, consts, out):
    with ExitStack() as ctx:
        def sb(name, shape, dt):
            return ctx.enter_context(nc.sbuf_tensor(name, shape, dt))

        def sem(name):
            return ctx.enter_context(nc.semaphore(name))

        cst = sb("cst", [P, C_ALL], F32)
        ident = cst[:, C_ID:C_ID + P]
        bias3 = sb("bias3", [P, 3 * DM], F32)
        bo_col = sb("bo_col", [P, KT], F32)
        w3_hi = sb("w3_hi", [P, KT, 3 * DM], F32R)
        w3_lo = sb("w3_lo", [P, KT, 3 * DM], F32R)
        wo_hi = sb("wo_hi", [P, KT, DM], F32R)
        wo_lo = sb("wo_lo", [P, KT, DM], F32R)
        wgu_hi = sb("wgu_hi", [P, 2, KT, HID], F32R)
        wgu_lo = sb("wgu_lo", [P, 2, KT, HID], F32R)
        wd_hi = sb("wd_hi", [P, HT, DM], F32R)
        wd_lo = sb("wd_lo", [P, HT, DM], F32R)
        xn = sb("xn", [P, TT, DM], F32)
        stats = sb("stats", [P, TT, 6], F32)
        mean_var = sb("mean_var", [P, TT, 2], F32)
        rstd = sb("rstd", [P, TT], F32)
        minus_half = sb("minus_half", [P, TT], F32)
        xt_hi = sb("xt_hi", [P, KT, SEQ], F32R)
        xt_lo = sb("xt_lo", [P, KT, SEQ], F32R)
        qk_raw = sb("qk_raw", [P, 2, 2 * DM], F32)
        rope_b = sb("rope_b", [P, 2 * DM], F32)
        rot = sb("rot", [P, 2, TT, 2 * DM], F32)
        vals = sb("vals", [P, 2, TT, 288], F32)
        q_nat = sb("q_nat", [P, 4, TT, 2, ST], F32)
        k_nat = sb("k_nat", [P, 2, TT, 2, ST], F32)
        q_st = sb("q_st", [P, 2, SEQ], F32R)
        q_st2 = sb("q_st2", [P, 2, SEQ], F32R)
        k_st = sb("k_st", [P, 4, SEQ], F32R)
        row_max = sb("row_max", [P, 2, TT, 2], F32)
        masked = sb("masked", [P, 2, SEQ], BF16)
        probs = sb("probs", [P, 2 * SLOTS, SEQ], F32)
        o_t = sb("o_t", [P, SEQ], F32)
        inv_sum = sb("inv_sum", [P, TT, 4], F32)
        attn = sb("attn", [P, TT, DM], F32)
        at_hi = sb("at_hi", [P, KT, SEQ], F32R)
        at_lo = sb("at_lo", [P, KT, SEQ], F32R)
        hid = sb("hid", [P, 2, SEQ], F32)
        h_hi = sb("h_hi", [P, HT, SEQ], F32R)
        h_lo = sb("h_lo", [P, HT, SEQ], F32R)
        gate = sb("gate", [P, 2, KT, SEQ], F32)
        res = sb("res", [P, TT, DM], F32)
        lo_sq = sb("lo_sq", [P, 12], F32)
        flag_i = sb("flag_i", [P, 1], I32)
        w3_raw = rot[:, 0, :, :].rearrange("p t c -> p (t c)")[:, 0:KT * 3 * DM].rearrange("p (k c) -> p k c", k=KT)
        wo_raw = rot[:, 1, :, :].rearrange("p t c -> p (t c)")[:, 0:KT * DM].rearrange("p (k c) -> p k c", k=KT)
        w_nat = probs[:, 0:9, :].rearrange("p (w a) c -> p w (a c)", w=3)

        ps_a = [ctx.enter_context(nc.psum_tensor(f"ps_a{i}", [P, SEQ], F32)) for i in range(2)]
        ps_b = [ctx.enter_context(nc.psum_tensor(f"ps_b{i}", [P, SEQ], F32)) for i in range(B_BANKS)]
        ps_o = ctx.enter_context(nc.psum_tensor("ps_o", [P, SEQ], F32))
        ps_w = [ctx.enter_context(nc.psum_tensor(f"ps_w{i}", [P, SEQ], F32)) for i in range(WORK_BANKS)]

        const_in = sem("const_in"); w3_in = sem("w3_in"); ffn_w_in = sem("ffn_w_in"); x_in = sem("x_in")
        res_in = sem("res_in"); out_stored = sem("out_stored")
        full = {"act": sem("work_full_for_act"), "dve": sem("work_full_for_dve")}
        w3_hi_ready = sem("w3_hi_ready"); w3_ready = sem("w3_ready"); ffn_w_float = sem("ffn_w_float")
        wt_hi = sem("wt_hi"); wt_ready = sem("wt_ready"); lo_squares = sem("lo_squares"); lo_max = sem("lo_max"); flag_set = sem("flag_set")
        dve_passed = sem("dve_passed"); pool_passed = sem("pool_passed")
        zeroed = sem("zeroed"); half_set = sem("half_set")
        stats_ready = sem("stats_ready"); aggr_ready = sem("aggr_ready"); rstd_ready = sem("rstd_ready")
        xn_ready = sem("xn_ready")
        xt_hi_ready = sem("xt_hi_ready"); xt_ready = sem("xt_ready")
        qk_ready = sem("qk_ready"); v_ready = sem("v_ready"); rope_parts = sem("rope_parts"); rot_ready = sem("rot_ready")
        hi_ready = sem("hi_ready"); lo_ready = sem("lo_ready")
        q_st_ready = sem("q_st_ready"); k_st_ready = sem("k_st_ready"); q_st2_ready = sem("q_st2_ready")
        a_full = sem("a_full"); a_taken = sem("a_taken"); max_hi = sem("max_hi"); max_ready = sem("max_ready")
        b_full = sem("b_full"); exp_done = sem("exp_done"); masked_done = sem("masked_done")
        pv_done = sem("pv_done"); o_t_ready = sem("o_t_ready"); inv_ready = sem("inv_ready"); attn_ready = sem("attn_ready")
        at_hi_ready = sem("at_hi_ready"); at_ready = sem("at_ready"); prod_ready = sem("prod_ready"); res_ready = sem("res_ready")
        tanh_ready = sem("tanh_ready"); gated = sem("gated"); hid_ready = sem("hid_ready")
        h_hi_ready = sem("h_hi_ready"); h_ready = sem("h_ready"); silu_ready = sem("silu_ready")
        released = {"T2": q_st2_ready, "T1q": q_st_ready, "T1k": k_st_ready, "XT": xt_ready, "QK": qk_ready, "V": v_ready,
                    "ON": attn_ready, "AT": at_ready, "OP": prod_ready, "FT": res_ready, "G": gated, "U": hid_ready,
                    "DN": silu_ready, "WT": wt_ready}

        bank = Bank()
        MIDDLE = (BATCH - 2) // 2

        def need(eng, s, value, per_batch, it, apart=None):
            if it is not None:
                assert value > 0
                wait = eng.wait_ge(s, it * (2 * per_batch) + value)
                if apart:
                    wait.then_inc(apart, 1)
            elif value > 0:
                eng.wait_ge(s, value)

        def run(eng, do):
            for item in plan(-1) + plan(0):
                do(item, None)
            with eng.Fori(0, MIDDLE) as it:
                for item in plan(1) + plan(2):
                    do(item, it)
            for item in plan(BATCH - 1) + epilogue_plan():
                do(item, None)

        def wait_full(eng, name, item, it):
            need(eng, full[name], bank.of[item][1], bank.full_per[name], it)

        def w_of(item):
            return ps_w[bank.of[item][0]]

        def wt_cols(i):
            return P * (2 if i < 8 and i % 2 else 4)

        def wt_view(gate_up, down, i):
            if i < 8:
                w, k, half = i // 4, i // 2 % 2, i % 2
                return gate_up[:, w, k, half * 512:half * 512 + wt_cols(i)]
            return down[:, 2 * (i - 8):2 * (i - 8) + 2, :].rearrange("p j d -> p (j d)")

        def tanh_at(b, j):
            return b * (HT + KT) + j + 1

        def rot_of(b, pair, which):
            c = which * DM + pair * 2 * HD
            return rot[:, b % 2, :, c:c + 2 * HD].rearrange("p t (h c) -> p t h c", h=2)

        CONST_LOADS = 1 + 3 + KT
        block = ctx.enter_context(nc.Block())

        @block.sync
        def _(sp):
            by_tile = lambda ap: ap.rearrange("(t p) d -> p t d", p=P)
            sp.dma_start(xn[:], by_tile(x[0])).then_inc(x_in, 16)
            for j, w in enumerate((wq, wk, wv)):
                sp.dma_start(w3_raw[:, :, j * DM:(j + 1) * DM], by_tile(w)).then_inc(w3_in, 16)
            sp.dma_start(wo_raw, by_tile(wo)).then_inc(w3_in, 16)
            sp.dma_start(cst[:], consts).then_inc(const_in, 16)
            for j, v in enumerate((bq, bk, bv)):
                sp.dma_start(bias3[:, j * DM:(j + 1) * DM],
                             v.rearrange("(a d) -> a d", a=1).broadcast_to([P, DM])).then_inc(const_in, 16)
            for k in range(KT):
                sp.dma_start(bo_col[:, k:k + 1], bo[k * P:(k + 1) * P].rearrange("(p a) -> p a", a=1)).then_inc(const_in, 16)
            for j, w in enumerate((w_gate, w_up)):
                sp.dma_start(w_nat[:, j, :].bitcast(I32).rearrange("p (t d) -> p t d", d=DM), by_tile(w)).then_inc(ffn_w_in, 16)
            sp.dma_start(w_nat[:, 2, :].bitcast(I32).rearrange("p (t d) -> p t d", d=HID), by_tile(w_down)).then_inc(ffn_w_in, 16)
            sp.dma_start(res[:], by_tile(x[0])).then_inc(res_in, 16)
            sp.wait_ge(xt_ready, KT)
            sp.dma_start(xn[:], by_tile(x[1])).then_inc(x_in, 16)
            with sp.Fori(1, BATCH - 1) as b:
                sp.wait_ge(xt_ready, b * KT + KT)
                sp.dma_start(xn[:], x[bass.ds(b + 1, 1), :, :].rearrange("a (t p) d -> p (a t) d", p=P)).then_inc(x_in, 16)
                sp.wait_ge(res_ready, b * 2)
                sp.dma_start(out[bass.ds(b - 1, 1), :, :].rearrange("a (t p) d -> p (a t) d", p=P), res[:]).then_inc(out_stored, 16)
                sp.wait_ge(out_stored, b * 16)
                sp.dma_start(res[:], x[bass.ds(b, 1), :, :].rearrange("a (t p) d -> p (a t) d", p=P)).then_inc(res_in, 16)
            for b in (BATCH - 2, BATCH - 1):
                sp.wait_ge(res_ready, (b + 1) * 2)
                sp.dma_start(by_tile(out[b]), res[:]).then_inc(out_stored, 16)
                sp.wait_ge(out_stored, (b + 1) * 16)
                if b + 1 < BATCH:
                    sp.dma_start(res[:], by_tile(x[b + 1])).then_inc(res_in, 16)

        @block.tensor
        def _(pe):
            flag = {}

            def take_bank(item, it):
                before = bank.of[item][2]
                if before:
                    need(pe, released[before[0]], before[1], bank.kind_per[before[0]], it)
                return w_of(item)

            def done(ins, item):
                ins.then_inc(full[WORK[item[0]][0]], 1)

            def group(dst, terms, middle=()):
                for i, (w, m) in enumerate(terms):
                    if middle and i == 1:
                        with pe.If(flag["has_lo"] > 0):
                            for wl, ml in middle:
                                pe.matmul(dst, wl, ml, start=False, stop=False)
                    last = pe.matmul(dst, w, m, start=(i == 0), stop=(i == len(terms) - 1))
                return last

            def do(item, it):
                kind, b, i = item
                n = b * PAIRS + i
                if kind == "WQ":
                    pe.wait_ge(const_in, 16 * CONST_LOADS)
                elif kind == "XT":
                    need(pe, xn_ready, (b + 1) * TT, TT, it)
                    dst = take_bank(item, it)
                    for tt in range(TT):
                        last = pe.transpose(dst[:, tt * P:(tt + 1) * P], xn[:, tt, i * P:(i + 1) * P], ident)
                    done(last, item)
                elif kind in ("QK", "V"):
                    if kind == "QK" and i == 0:
                        need(pe, xt_ready, (b + 1) * KT, KT, it)
                        if b == 0:
                            pe.wait_ge(w3_ready, 2)
                    dst = take_bank(item, it)
                    c0, c1 = (0, 2 * DM) if kind == "QK" else (2 * DM, 3 * DM)
                    tok = slice(i * P, (i + 1) * P)
                    terms = []
                    for k in range(KT):
                        terms += [(xt_hi[:, k, tok], w3_hi[:, k, c0:c1]), (xt_hi[:, k, tok], w3_lo[:, k, c0:c1]),
                                  (xt_lo[:, k, tok], w3_hi[:, k, c0:c1])]
                    done(group(dst[:, 0:c1 - c0], terms), item)
                elif kind == "WT":
                    if i == 0:
                        pe.wait_ge(ffn_w_float, 3)
                    dst = take_bank(item, it)
                    if i < 8:
                        w, k, half = i // 4, i // 2 % 2, i % 2
                        for a, t in enumerate(range(4 * half, min(4 * half + 4, HT))):
                            last = pe.transpose(dst[:, a * P:(a + 1) * P], w_nat[:, w, t * DM + k * P:t * DM + (k + 1) * P], ident)
                    else:
                        for a, (j, m) in enumerate([(2 * (i - 8) + jj, m) for jj in range(2) for m in range(KT)]):
                            last = pe.transpose(dst[:, a * P:(a + 1) * P], w_nat[:, 2, m * HID + j * P:m * HID + (j + 1) * P], ident)
                    done(last, item)
                elif kind == "FLAG":
                    pe.wait_ge(flag_set, 1)
                    flag["has_lo"] = pe.value_load(flag_i[0:1, 0:1], min_val=0, max_val=1)
                elif kind in ("T1q", "T1k"):
                    if kind == "T1q":
                        need(pe, lo_ready, 2 * (n + 1), 2 * PAIRS, it)
                    dst = take_bank(item, it)
                    for tt in range(TT):
                        src = (q_nat[:, i % 4, tt] if kind == "T1q" else k_nat[:, i % 2, tt]).rearrange("p h c -> p (h c)")
                        last = pe.transpose(dst[:, tt * P:(tt + 1) * P], src, ident)
                    done(last, item)
                elif kind == "T2":
                    need(pe, max_ready, n + 1, PAIRS, it)
                    dst = take_bank(item, it)
                    for tt in range(TT):
                        last = pe.transpose(dst[:, tt * P:(tt + 1) * P], q_nat[:, i % 4, tt].rearrange("p h c -> p (h c)"), ident)
                    done(last, item)
                elif kind == "A":
                    pair, c = divmod(i, CHUNKS)
                    m = b * PAIRS * CHUNKS + i
                    if c == 0:
                        need(pe, q_st_ready, b * PAIRS + pair + 1, PAIRS, it)
                        need(pe, k_st_ready, b * PAIRS + pair + 1, PAIRS, it)
                    need(pe, a_taken, m - 1, PAIRS * CHUNKS, it)
                    for h, qt, col in A_PARTS[c]:
                        rows = slice(h * ST, h * ST + 3 * HD)
                        w = (qt + 1) * P
                        last = pe.matmul(ps_a[i % 2][:, col:col + w], q_st[rows, pair % 2, qt * P:(qt + 1) * P],
                                         k_st[rows, pair % 4, 0:w], start=True, stop=True)
                    last.then_inc(a_full, 1)
                elif kind == "B":
                    pair, c = divmod(i, CHUNKS)
                    if c == 0:
                        need(pe, q_st2_ready, b * PAIRS + pair + 1, PAIRS, it)
                    per = PAIRS * CHUNKS
                    need(pe, exp_done, b * per + i + 1 - B_BANKS, per, it)
                    for h, kt, col in B_PARTS[c]:
                        rows = slice(h * ST, (h + 1) * ST)
                        w = SEQ - kt * P
                        last = pe.matmul(ps_b[i % B_BANKS][:, col:col + w], k_st[rows, pair % 4, kt * P:(kt + 1) * P],
                                         q_st2[rows, pair % 2, kt * P:SEQ], start=True, stop=True)
                    last.then_inc(b_full, 1)
                elif kind == "PV":
                    group_, step = divmod(i, TT)
                    g, kt = b * GROUPS + group_, PV_ORDER[step]
                    if step == 0:
                        need(pe, o_t_ready, g, GROUPS, it)
                        need(pe, v_ready, (b + 1) * TT, TT, it)
                    if step != 2:
                        need(pe, masked_done, CHUNKS * (2 * g + 1) + (2, 4, 0, 6)[step], PAIRS * CHUNKS, it)
                    for hh in range(4):
                        slot, col = P_AT[kt][hh % 2]
                        head = 4 * group_ + hh
                        last = pe.matmul(ps_o[32 * hh:32 * hh + 32, kt * P:SEQ],
                                         vals[:, b % 2, kt, head * VW:head * VW + 32],
                                         probs[:, (hh // 2) * SLOTS + slot, col:col + SEQ - kt * P],
                                         start=(step == 0), stop=(step == TT - 1), skip_group_check=True)
                    last.then_inc(pv_done, 1)
                elif kind == "ON":
                    need(pe, o_t_ready, b * GROUPS + i + 1, GROUPS, it)
                    dst = take_bank(item, it)
                    for tt in range(TT):
                        last = pe.transpose(dst[:, tt * P:(tt + 1) * P], o_t[:, tt * P:(tt + 1) * P], ident)
                    done(last, item)
                elif kind == "AT":
                    need(pe, attn_ready, (b + 1) * GROUPS, GROUPS, it)
                    dst = take_bank(item, it)
                    for tt in range(TT):
                        last = pe.transpose(dst[:, tt * P:(tt + 1) * P], attn[:, tt, i * P:(i + 1) * P], ident)
                    done(last, item)
                elif kind == "OP":
                    need(pe, at_ready, (b + 1) * KT, KT, it)
                    dst = take_bank(item, it)
                    col = slice(i * P, (i + 1) * P)
                    terms = []
                    for k in range(KT):
                        terms += [(wo_hi[:, k, col], at_hi[:, k, :]), (wo_lo[:, k, col], at_hi[:, k, :]),
                                  (wo_hi[:, k, col], at_lo[:, k, :])]
                    done(group(dst[:, :], terms), item)
                elif kind == "FT":
                    need(pe, prod_ready, (b + 1) * KT, KT, it)
                    dst = take_bank(item, it)
                    for a, (tt, m) in enumerate([(2 * i + t, m) for t in range(2) for m in range(KT)]):
                        last = pe.transpose(dst[:, a * P:(a + 1) * P], hid[:, m, tt * P:(tt + 1) * P], ident)
                    done(last, item)
                elif kind in ("G", "U"):
                    if kind == "G" and i == 0:
                        need(pe, xt_ready, (b + 1) * KT, KT, it)
                    dst = take_bank(item, it)
                    w, col = (0 if kind == "G" else 1), slice(i * P, (i + 1) * P)
                    terms = [(wgu_hi[:, w, k, col], xt[:, k, :]) for k in range(KT) for xt in (xt_hi, xt_lo)]
                    low = [(wgu_lo[:, w, k, col], xt_hi[:, k, :]) for k in range(KT)]
                    done(group(dst[:, :], terms, low), item)
                elif kind == "DN":
                    need(pe, h_ready, (b + 1) * HT, HT, it)
                    dst = take_bank(item, it)
                    col = slice(i * P, (i + 1) * P)
                    terms = [(wd_hi[:, j, col], h[:, j, :]) for j in range(HT) for h in (h_hi, h_lo)]
                    low = [(wd_lo[:, j, col], h_hi[:, j, :]) for j in range(HT)]
                    done(group(dst[:, :], terms, low), item)

            run(pe, do)

        @block.scalar
        def _(act):
            def do(item, it):
                kind, b, i = item
                n = b * PAIRS + i
                if kind == "WQ":
                    act.wait_ge(w3_in, 64)
                    nc.scalar.copy(w3_hi[:], w3_raw).then_inc(w3_hi_ready, 1)
                    nc.scalar.copy(wo_hi[:], wo_raw).then_inc(w3_hi_ready, 1)
                elif kind == "XT":
                    wait_full(act, "act", item, it)
                    nc.scalar.copy(xt_hi[:, i, :], w_of(item)[:, :]).then_inc(xt_hi_ready, 1)
                elif kind == "WT":
                    wait_full(act, "act", item, it)
                    nc.scalar.copy(wt_view(wgu_hi, wd_hi, i), w_of(item)[:, 0:wt_cols(i)]).then_inc(wt_hi, 1)
                elif kind in ("T1q", "T1k", "T2"):
                    wait_full(act, "act", item, it)
                    dst, ready = {"T1q": (q_st[:, i % 2, :], q_st_ready), "T1k": (k_st[:, i % 4, :], k_st_ready),
                                  "T2": (q_st2[:, i % 2, :], q_st2_ready)}[kind]
                    nc.scalar.copy(dst, w_of(item)[:, :]).then_inc(ready, 1)
                elif kind == "B":
                    pair, c = divmod(i, CHUNKS)
                    m = b * PAIRS * CHUNKS + i
                    need(act, b_full, m + 1, PAIRS * CHUNKS, it)
                    if pair % 2 == 0:
                        need(act, pv_done, TT * ((b * PAIRS + pair) // 2 - 1) + (1, 1, 3, 3, 4, 4)[c], TT * GROUPS, it)
                    slot, col = slot_of(c)
                    nc.scalar.activation(probs[:, (pair % 2) * SLOTS + slot, col:col + WIDTH[c]], ps_b[i % B_BANKS][:, 0:WIDTH[c]], ACT.Exp,
                                         scale=QSCALE).then_inc(exp_done, 1)
                elif kind == "PV" and i % TT == TT - 1:
                    need(act, pv_done, b * GROUPS * TT + i + 1, GROUPS * TT, it)
                    nc.scalar.copy(o_t[:, :], ps_o[:, :]).then_inc(o_t_ready, 1)
                elif kind == "AT":
                    wait_full(act, "act", item, it)
                    nc.scalar.copy(at_hi[:, i, :], w_of(item)[:, :]).then_inc(at_hi_ready, 1)
                elif kind == "G":
                    wait_full(act, "act", item, it)
                    if i >= 2:
                        need(act, h_ready, b * HT + i - 1, HT, it)
                    elif b:
                        need(act, silu_ready, b * KT, KT, it)
                    nc.scalar.activation(hid[:, i % 2, :], w_of(item)[:, :], ACT.Tanh,
                                         scale=0.5 * WSCALE).then_inc(tanh_ready, 1)
                elif kind == "HL":
                    need(act, hid_ready, b * HT + i + 1, HT, it)
                    nc.scalar.copy(h_hi[:, i, :], hid[:, i % 2, :]).then_inc(h_hi_ready, 1)
                elif kind == "DN":
                    wait_full(act, "act", item, it)
                    nc.scalar.activation(hid[:, i, :], w_of(item)[:, :], ACT.Tanh,
                                         scale=0.5 * WSCALE).then_inc(tanh_ready, 1)

            run(act, do)

        @block.vector
        def _(dve):
            def do(item, it):
                kind, b, i = item
                n = b * PAIRS + i
                if kind == "WQ":
                    nc.vector.memset(q_nat[:], 0.0).then_inc(zeroed, 1)
                    nc.vector.memset(k_nat[:], 1.0).then_inc(zeroed, 1)
                    nc.vector.memset(vals[:], 1.0).then_inc(zeroed, 1)
                    nc.vector.memset(lo_sq[:], 0.0).then_inc(zeroed, 1)
                    dve.wait_ge(w3_hi_ready, 2)
                    nc.vector.tensor_tensor(w3_lo[:], w3_raw, w3_hi[:].bitcast(F32), ALU.subtract).then_inc(w3_ready, 1)
                    nc.vector.tensor_tensor(wo_lo[:], wo_raw, wo_hi[:].bitcast(F32), ALU.subtract).then_inc(w3_ready, 1)
                    dve.wait_ge(ffn_w_in, 48)
                    for w in range(3):
                        nc.vector.tensor_copy(w_nat[:, w, :], w_nat[:, w, :].bitcast(I32)).then_inc(ffn_w_float, 1)
                    dve.wait_ge(const_in, 16 * CONST_LOADS)
                    dve.wait_ge(zeroed, 4)
                elif kind == "LN":
                    need(dve, x_in, 16 * (b + 1), 16, it)
                    need(dve, aggr_ready, TT * b, TT, it)
                    for tt in range(TT):
                        nc.vector.bn_stats(stats[:, tt, :], xn[:, tt, :]).then_inc(stats_ready, 1)
                    need(dve, stats_ready, TT * (b + 1), TT, it, apart=dve_passed)
                    for tt in range(TT):
                        nc.vector.bn_aggr(mean_var[:, tt, :], stats[:, tt, :]).then_inc(aggr_ready, 1)
                elif kind == "XT":
                    need(dve, xt_hi_ready, b * KT + i + 1, KT, it)
                    nc.vector.tensor_tensor(xt_lo[:, i, :], w_of(item)[:, :], xt_hi[:, i, :].bitcast(F32), ALU.subtract)\
                        .then_inc(xt_ready, 1)
                elif kind == "QK":
                    wait_full(dve, "dve", item, it)
                    need(dve, rot_ready, b * TT + i - 1, TT, it)
                    nc.vector.tensor_tensor(qk_raw[:, i % 2, :], w_of(item)[:, :], bias3[:, 0:2 * DM], ALU.add)\
                        .then_inc(qk_ready, 1)
                elif kind == "V":
                    wait_full(dve, "dve", item, it)
                    v3 = vals[:, b % 2, i, 0:HEADS * VW].rearrange("p (h c) -> p h c", c=VW)[:, :, 0:HD]
                    nc.vector.tensor_tensor(v3, w_of(item)[:, 0:DM].rearrange("p (h c) -> p h c", c=HD),
                                            bias3[:, 2 * DM:3 * DM].rearrange("p (h c) -> p h c", c=HD), ALU.add)\
                        .then_inc(v_ready, 1)
                elif kind == "WT":
                    dve.wait_ge(wt_hi, i + 1)
                    hi, lo = wt_view(wgu_hi, wd_hi, i), wt_view(wgu_lo, wd_lo, i)
                    nc.vector.tensor_tensor(lo, w_of(item)[:, 0:wt_cols(i)], hi.bitcast(F32), ALU.subtract)\
                        .then_inc(wt_ready, 1)
                elif kind == "FLAG":
                    dve.wait_ge(wt_ready, WT_USES)
                    for w in range(WT_USES):
                        lo = wt_view(wgu_lo, wd_lo, w).bitcast(F32)
                        if w:
                            dve.wait_ge(lo_squares, w)
                        nc.vector.tensor_tensor_reduce(out=masked[:, 0, 0:wt_cols(w)], in0=lo, in1=lo, scale=1.0, scalar=0.0,
                                                       op0=ALU.mult, op1=ALU.max, accum_out=lo_sq[:, w:w + 1])\
                            .then_inc(lo_squares, 1)
                    dve.wait_ge(lo_squares, WT_USES)
                    nc.vector.tensor_reduce(lo_sq[:, 11:12], lo_sq[:, 0:WT_USES], AX.X, ALU.max).then_inc(lo_squares, 1)
                    dve.wait_ge(lo_max, 1)
                    nc.vector.tensor_scalar(flag_i[:], lo_sq[:, 0:1], 0.0, None, ALU.is_gt).then_inc(flag_set, 1)
                elif kind == "LO":
                    need(dve, hi_ready, 4 * (n + 1), 4 * PAIRS, it)
                    qn, kn = q_nat[:, i % 4, :, :, :], k_nat[:, i % 2, :, :, :]
                    nc.vector.tensor_tensor(qn[:, :, :, 2 * HD:3 * HD], rot_of(b, i, 0), qn[:, :, :, 0:HD], ALU.subtract)\
                        .then_inc(lo_ready, 1)
                    nc.vector.tensor_tensor(kn[:, :, :, HD:2 * HD], rot_of(b, i, 1), kn[:, :, :, 0:HD], ALU.subtract)\
                        .then_inc(lo_ready, 1)
                elif kind == "A":
                    pair, c = divmod(i, CHUNKS)
                    m = b * PAIRS * CHUNKS + i
                    if c == 0:
                        need(dve, max_ready, b * PAIRS + pair - 1, PAIRS, it)
                    need(dve, a_taken, m - 1, PAIRS * CHUNKS, it)
                    need(dve, a_full, m + 1, PAIRS * CHUNKS, it, apart=dve_passed)
                    for h, qt, col in A_PARTS[c]:
                        w = (qt + 1) * P
                        last = nc.vector.tensor_tensor_reduce(
                            out=masked[:, i % 2, col:col + w], in0=ps_a[i % 2][:, col:col + w], in1=cst[:, C_MASK + SEQ - w:C_MASK + SEQ],
                            scale=1.0, scalar=-3e38, op0=ALU.add, op1=ALU.max, accum_out=row_max[:, pair % 2, qt, h:h + 1])
                    last.then_inc(a_taken, 1)
                elif kind == "MX":
                    need(dve, a_taken, (n + 1) * CHUNKS, PAIRS * CHUNKS, it)
                    mx, qn = row_max[:, i % 2, :, :], q_nat[:, i % 4, :, :, :]
                    nc.vector.tensor_scalar(qn[:, :, :, 3 * HD].bitcast(F32R), mx, -1.0, None, ALU.mult).then_inc(max_hi, 1)
                    need(dve, max_hi, n + 1, PAIRS, it)
                    nc.vector.scalar_tensor_tensor(out=qn[:, :, :, 3 * HD + 1], in0=mx, scalar=-1.0, in1=qn[:, :, :, 3 * HD],
                                                   op0=ALU.mult, op1=ALU.subtract).then_inc(max_ready, 1)
                elif kind == "ON":
                    wait_full(dve, "dve", item, it)
                    o4 = w_of(item)[:, :].rearrange("p (t h c) -> p t h c", t=TT, h=4)
                    g = b * GROUPS + i
                    need(dve, attn_ready, g, GROUPS, it)
                    nc.vector.reciprocal(inv_sum[:], o4[:, :, :, HD]).then_inc(inv_ready, 1)
                    need(dve, inv_ready, g + 1, GROUPS, it)
                    nc.vector.tensor_tensor(attn[:, :, i * 64:(i + 1) * 64].rearrange("p t (h c) -> p t h c", h=4),
                                            o4[:, :, :, 0:HD], inv_sum[:].rearrange("p t (h a) -> p t h a", a=1)
                                            .broadcast_to([P, TT, 4, HD]), ALU.mult).then_inc(attn_ready, 1)
                elif kind == "AT":
                    need(dve, at_hi_ready, b * KT + i + 1, KT, it)
                    nc.vector.tensor_tensor(at_lo[:, i, :], w_of(item)[:, :], at_hi[:, i, :].bitcast(F32), ALU.subtract)\
                        .then_inc(at_ready, 1)
                elif kind == "OP":
                    wait_full(dve, "dve", item, it)
                    nc.vector.scalar_tensor_tensor(out=hid[:, i, :], in0=w_of(item)[:, :], scalar=bo_col[:, i:i + 1],
                                                   in1=gate[:, b % 2, i, :], op0=ALU.add, op1=ALU.mult).then_inc(prod_ready, 1)
                elif kind == "FT":
                    wait_full(dve, "dve", item, it)
                    if i == 0:
                        need(dve, res_in, 16 * (b + 1), 16, it)
                    r = res[:, 2 * i:2 * i + 2, :].rearrange("p t d -> p (t d)")
                    nc.vector.scalar_tensor_tensor(out=r, in0=w_of(item)[:, :], scalar=0.5 * WSCALE, in1=r,
                                                   op0=ALU.mult, op1=ALU.add).then_inc(res_ready, 1)
                elif kind == "G":
                    need(dve, tanh_ready, tanh_at(b, i), HT + KT, it)
                    nc.vector.scalar_tensor_tensor(out=hid[:, i % 2, :], in0=hid[:, i % 2, :], scalar=1.0,
                                                   in1=w_of(item)[:, :], op0=ALU.add, op1=ALU.mult).then_inc(gated, 1)
                elif kind == "U":
                    wait_full(dve, "dve", item, it)
                    need(dve, gated, b * HT + i + 1, HT, it)
                    nc.vector.scalar_tensor_tensor(out=hid[:, i % 2, :], in0=w_of(item)[:, :], scalar=0.5 * WSCALE * WSCALE,
                                                   in1=hid[:, i % 2, :], op0=ALU.mult, op1=ALU.mult).then_inc(hid_ready, 1)
                elif kind == "HL":
                    need(dve, h_hi_ready, b * HT + i + 1, HT, it)
                    nc.vector.tensor_tensor(h_lo[:, i, :], hid[:, i % 2, :], h_hi[:, i, :].bitcast(F32), ALU.subtract)\
                        .then_inc(h_ready, 1)
                elif kind == "DN":
                    need(dve, tanh_ready, tanh_at(b, HT + i), HT + KT, it)
                    nc.vector.scalar_tensor_tensor(out=gate[:, b % 2, i, :], in0=hid[:, i, :], scalar=1.0,
                                                   in1=w_of(item)[:, :], op0=ALU.add, op1=ALU.mult).then_inc(silu_ready, 1)

            run(dve, do)

        @block.gpsimd
        def _(pool):
            def do(item, it):
                kind, b, i = item
                n = b * PAIRS + i
                if kind == "WQ":
                    pool.wait_ge(const_in, 16 * CONST_LOADS)
                    nc.gpsimd.memset(minus_half[:], -0.5).then_inc(half_set, 1)
                    pool.wait_ge(half_set, 1)
                    pool.wait_ge(zeroed, 4)
                elif kind == "LN":
                    need(pool, xn_ready, TT * b, TT, it)
                    need(pool, aggr_ready, TT * (b + 1), TT, it, apart=pool_passed)
                    nc.gpsimd.tensor_scalar(rstd[:], mean_var[:, :, 1], EPS, None, ALU.add).then_inc(rstd_ready, 1)
                    need(pool, rstd_ready, 2 * b + 1, 2, it)
                    nc.gpsimd.tensor_tensor(rstd[:], rstd[:], minus_half[:], ALU.pow).then_inc(rstd_ready, 1)
                    need(pool, rstd_ready, 2 * b + 2, 2, it, apart=pool_passed)
                    for tt in range(TT):
                        nc.gpsimd.tensor_scalar(xn[:, tt, :], xn[:, tt, :], mean_var[:, tt, 0:1], rstd[:, tt:tt + 1],
                                                ALU.subtract, ALU.mult).then_inc(xn_ready, 1)
                elif kind == "ROPE":
                    t, part = divmod(i, 4)
                    src, dst = qk_raw[:, t % 2, :], rot[:, b % 2, t, :]
                    by_head = lambda ap: ap.rearrange("p (h c) -> p h c", c=HD)
                    by_two = lambda ap: ap.rearrange("p (h j e) -> p h j e", j=HD // 2, e=2)
                    cos = cst[:, C_COS + t * HD:C_COS + (t + 1) * HD].rearrange("p (a c) -> p a c", a=1).broadcast_to([P, 2 * HEADS, HD])
                    sin = cst[:, C_SIN + t * HD:C_SIN + (t + 1) * HD].rearrange("p (a j e) -> p a j e", a=1, e=2)\
                        .broadcast_to([P, 2 * HEADS, HD // 2, 2])
                    if part == 0:
                        need(pool, qk_ready, b * TT + t + 1, TT, it)
                        nc.gpsimd.tensor_tensor(by_head(dst), by_head(src), cos, ALU.mult).then_inc(rope_parts, 1)
                    elif part < 3:
                        e = part - 1
                        if e == 0:
                            need(pool, rot_ready, b * TT + t, TT, it)
                        nc.gpsimd.tensor_tensor(by_two(rope_b[:])[:, :, :, e], by_two(src)[:, :, :, 1 - e], sin[:, :, :, e],
                                                ALU.mult).then_inc(rope_parts, 1)
                    else:
                        need(pool, rope_parts, 3 * (b * TT + t + 1), 3 * TT, it)
                        nc.gpsimd.tensor_tensor(dst, dst, rope_b[:], ALU.add).then_inc(rot_ready, 1)
                elif kind == "HI":
                    need(pool, rot_ready, (b + 1) * TT, TT, it)
                    need(pool, q_st2_ready, n - 3, PAIRS, it)
                    need(pool, k_st_ready, n - 1, PAIRS, it, apart=pool_passed)
                    qn, kn = q_nat[:, i % 4], k_nat[:, i % 2]
                    for nat, which, places in ((qn, 0, (0, 1)), (kn, 1, (0, 2))):
                        for at in places:
                            nc.gpsimd.tensor_copy(nat[:, :, :, at * HD:(at + 1) * HD].bitcast(F32R), rot_of(b, i, which))\
                                .then_inc(hi_ready, 1)
                elif kind == "B":
                    pair, c = divmod(i, CHUNKS)
                    m = b * PAIRS * CHUNKS + i
                    need(pool, exp_done, m + 1, PAIRS * CHUNKS, it, apart=pool_passed)
                    blocks = [col for _, _, col in B_PARTS[c]]
                    slot, col = slot_of(c)
                    pr = probs[:, (pair % 2) * SLOTS + slot, col:col + WIDTH[c]]
                    if len(blocks) == 1:
                        v, pattern = pr[:, 0:P], [[1, P]]
                    else:
                        a = pr[:, 0:P]
                        ap = list(a.ap)
                        v = bass.AP(tensor=a.tensor, offset=a.offset, ap=[list(ap[0]), [blocks[1], 2], [1, P]])
                        pattern = [[0, 2], [1, P]]
                    nc.gpsimd.affine_select(out=v, in_=v, compare_op=ALU.is_ge, fill=0.0, base=0, pattern=pattern,
                                            channel_multiplier=-1).then_inc(masked_done, 1)
                elif kind == "FLAG":
                    pool.wait_ge(lo_squares, WT_USES + 1)
                    nc.gpsimd.partition_all_reduce(lo_sq[:, 0:1], lo_sq[:, 11:12], P, bass.bass_isa.ReduceOp.max).then_inc(lo_max, 1)

            run(pool, do)


_INS = ["L0_attn_x", "L0_attn_wq", "L0_attn_bq", "L0_attn_wk", "L0_attn_bk", "L0_attn_wv", "L0_attn_bv", "L0_attn_wo",
        "L0_attn_bo", "L0_ffn_w_gate", "L0_ffn_w_up", "L0_ffn_w_down"]


def kernel(**inputs):
    import concourse.bacc as bacc
    from concourse.bass_utils import run_bass_kernel_spmd

    nc = bacc.Bacc("TRN2", target_bir_lowering=False, num_devices=1)
    arrays = {name: np.ascontiguousarray(inputs[name]) for name in _INS}
    arrays["shape_constants"] = shape_constants()
    args = [nc.dram_tensor(name, a.shape, mybir.dt.from_np(a.dtype), kind="ExternalInput").ap()
            for name, a in arrays.items()]
    result = nc.dram_tensor("result", (BATCH, SEQ, DM), F32, kind="ExternalOutput").ap()
    build(nc, *args, result)
    r = run_bass_kernel_spmd(nc, [arrays], core_ids=[0])
    return r.results[0]["result"]
```

```python
from contextlib import ExitStack

import numpy as np

import concourse.bass as bass
from concourse import mybir

ALU = mybir.AluOpType
ACT = mybir.ActivationFunctionType
AX = mybir.AxisListType
F32 = mybir.dt.float32
F32R = mybir.dt.float32r
I32 = mybir.dt.int32
BF16 = mybir.dt.bfloat16

P = 128
BATCH, SEQ, DM = 8, 512, 256
HEADS, HD = 16, 16
HID = 768
TT = SEQ // P
KT = DM // P
HT = HID // P
PAIRS = HEADS // 2
GROUPS = HEADS // 4
ST = 4 * HD
VW = HD + 1
CHUNKS = 6
SLOTS = 5
WEIGHTS_AT, WEIGHTS_STEP = 11, 1
WORK_BANKS, B_BANKS = 3, 2
HI_ENGINE = {"HIq": "act", "HIk": "pool"}
QSCALE = float(HD) ** -0.5
WSCALE = 1.0 / 127.0
EPS = 1e-5
NEG = -1e9 / QSCALE

C_ID, C_MASK, C_COS, C_SIN = 0, P, P + SEQ, P + SEQ + TT * HD
C_ALL = C_SIN + TT * HD


def shape_constants():
    inv_freq = (np.float32(1.0) / np.float32(10000.0) ** (np.arange(0, HD, 2, dtype=np.float32) / np.float32(HD)))
    freqs = np.arange(SEQ, dtype=np.float32)[:, None] * inv_freq.astype(np.float32)[None, :]
    cos, sin = np.cos(freqs), np.sin(freqs)
    cos2 = np.repeat(cos, 2, axis=1)
    sin2 = np.stack([-sin, sin], axis=-1).reshape(SEQ, HD)
    by_tile = lambda t: t.reshape(TT, P, HD).transpose(1, 0, 2).reshape(P, TT * HD)
    mask = np.zeros((P, SEQ), np.float32)
    mask[:, SEQ - P:] = np.where(np.arange(P)[None, :] > np.arange(P)[:, None], NEG, 0.0)
    return np.concatenate([np.eye(P, dtype=np.float32), mask, by_tile(cos2), by_tile(sin2)], axis=1).astype(np.float32)


B_PARTS = [[(h, kt, col) for kt, col in part] for part in ([(0, 0)], [(1, 0), (3, 384)], [(2, 0)]) for h in range(2)]
A_PARTS = [[(h, TT - 1 - kt, col) for h, kt, col in part] for part in B_PARTS]
WIDTH = [SEQ, SEQ, SEQ, SEQ, SEQ // 2, SEQ // 2]


def slot_of(c):
    return (c, 0) if c < 4 else (4, (c - 4) * (SEQ // 2))


P_AT = [[next((slot_of(c)[0], slot_of(c)[1] + col) for c, parts in enumerate(B_PARTS) for hh, k, col in parts
              if (hh, k) == (h, kt)) for h in range(2)] for kt in range(TT)]
PV_ORDER = [0, 1, 3, 2]

WORK = {"T2": ("act", "q_st2_ready"), "T1q": ("act", "q_st_ready"), "T1k": ("act", "k_st_ready"),
        "XT": ("act", "xt_ready"), "QK": ("dve", "qk_ready"), "V": ("dve", "v_ready"), "ON": ("dve", "attn_ready"),
        "AT": ("act", "at_ready"), "OP": ("dve", "prod_ready"), "FT": ("dve", "res_ready"), "G": ("act", "gated"),
        "U": ("dve", "hid_ready"), "DN": ("act", "silu_ready"), "WT": ("act", "wt_ready")}
WT_USES = 11


AHEAD = {"B": -1, "T2": 0, "A": 1, "MX": 1, "T1q": 2, "T1k": 2, "HIq": 3, "HIk": 3, "LOq": 3, "LOk": 3}

SCHEDULE = [line.split() for line in """
B0 A0 B1 ON2< B2 A1 ST0> RS0> T1q A2 HIq NM0> G5 B3 HIk NM1> A3 U5 T1k PV12< HL4 NM2> B4 NM3> A4 HL5 LOk T2 LOq A5 B5 PV13< DN0 MX
HIq B0 PV14< B1 A0 A1 DN1 PV15< T1q B2 A2 B3 HIk T1k B4 A3 A4 XT0> T2 LOq B5 LOk A5 XT1> MX
A0 B0 V0> B1 QK0> HIk ROPE0> A1 B2 A2 ROPE1> T1q HIq ROPE2> B3 V1> ROPE3> LOk A3 ON3< A4 QK1> B4 ROPE4> T2 T1k A5 B5 PV0 PV1 ROPE5> ROPE6> ROPE7> MX LOq
PV2 A0 B0 B1 AT0< A1 AT1< PV3 T1q A2 HIq B2 B3 T1k HIk A3 QK2> A4 ROPE8> B4 LOq ROPE9> LOk T2 A5 V2> B5 ROPE10> MX
B0 A0 QK3> B1 ROPE11> A1 B2 A2 T1q ROPE12> HIq B3 V3> ROPE13> HIk ROPE14> A3 PV4 T1k ROPE15> LOq B4 A4 T2 B5 A5 OP0< PV5 OP1< ON0 MX LOk
PV6 B0 B1 A0 FT0< A1 HIq T1q B2 A2 B3 HIk PV7 FT1< A3 T1k LOq A4 G0> T2 B4 B5 LOk A5 U0> MX
A0 ON1 B0 B1 A1 G1> B2 T1q A2 HIq U1> B3 HL0> A3 HIk T1k G2> PV8 A4 U2> B4 LOk LOq T2 A5 B5 HL1> MX
PV9 PV10 B0 B1 A0 A1 G3> PV11 T1q B2 HIq U3> A2 B3 HIk HL2> T1k A3 G4> A4 B4 LOq T2 B5 LOk U4> A5 HL3> MX
""".strip().splitlines()]


def steps(b):
    items = []
    for s, line in enumerate(SCHEDULE):
        for token in line:
            name = token.rstrip("<>")
            kind = name.rstrip("0123456789") if name not in ("T1q", "T1k", "T2") else name
            index = int(name[len(kind):] or 0)
            if kind in AHEAD:
                n = b * PAIRS + s + AHEAD[kind]
                items.append((kind, n // PAIRS, n % PAIRS * (CHUNKS if kind in "AB" else 1) + index))
            else:
                items.append((kind, b + token.count(">") - token.count("<"), index))
    return items


def plan(b):
    items = [item for item in steps(b) if 0 <= item[1] < BATCH]
    if b < 0:
        weights = [("WT", 0, i) for i in range(WT_USES)] + [("FLAG", 0, 0)]
        cut, end = min(items.index(("QK", 0, 0)), items.index(("V", 0, 0))), items.index(("G", 0, 0))
        mixed = [("WC", 0, 0)] + items[cut:end]
        for k, item in enumerate(weights):
            mixed.insert(WEIGHTS_AT + (WEIGHTS_STEP + 1) * k, item)
        items = [("WQ", 0, 0)] + items[:cut] + mixed + items[end:]
    return items


class Bank:

    def __init__(self):
        self.of, full, kinds, seen = {}, {"act": 0, "dve": 0}, {}, {}
        for b in range(-1, BATCH + 1):
            segment = plan(b)
            places = [i for i in (steps(b) if b >= 0 else segment) if i[0] in WORK]
            for item in segment:
                if item[0] in WORK:
                    kind, first = item[0], WORK[item[0]][0]
                    at = places.index(item) % WORK_BANKS
                    full[first] += 1
                    kinds[kind] = kinds.get(kind, 0) + 1
                    self.of[item] = (at, full[first], seen.get(at))
                    seen[at] = (kind, kinds[kind])
        middle = [i[0] for i in plan(2) if i[0] in WORK]
        self.full_per = {e: sum(WORK[k][0] == e for k in middle) for e in full}
        self.kind_per = {k: middle.count(k) for k in WORK}
        for one, two in zip(plan(1) + plan(2), plan(3) + plan(4)):
            if one[0] in WORK:
                a, b = self.of[one], self.of[two]
                assert a[0] == b[0] and b[1] - a[1] == 2 * self.full_per[WORK[one[0]][0]]
                assert a[2][0] == b[2][0] and b[2][1] - a[2][1] == 2 * self.kind_per[a[2][0]]


def build(nc, x, wq, bq, wk, bk, wv, bv, wo, bo, w_gate, w_up, w_down, consts, out):
    with ExitStack() as ctx:
        def sb(name, shape, dt):
            return ctx.enter_context(nc.sbuf_tensor(name, shape, dt))

        def sem(name):
            return ctx.enter_context(nc.semaphore(name))

        cst = sb("cst", [P, C_ALL], F32)
        ident = cst[:, C_ID:C_ID + P]
        ident_r = sb("ident_r", [P, P], F32R)
        bias3 = sb("bias3", [P, 3 * DM], F32)
        bo_col = sb("bo_col", [P, KT], F32)
        w3_hi = sb("w3_hi", [P, KT, 3 * DM], F32R)
        w3_lo = sb("w3_lo", [P, KT, 3 * DM], F32R)
        wo_hi = sb("wo_hi", [P, KT, DM], F32R)
        wo_lo = sb("wo_lo", [P, KT, DM], F32R)
        wgu_hi = sb("wgu_hi", [P, 2, KT, HID], F32R)
        wgu_lo = sb("wgu_lo", [P, 2, KT, HID], F32R)
        wd_hi = sb("wd_hi", [P, HT, DM], F32R)
        wd_lo = sb("wd_lo", [P, HT, DM], F32R)
        xn = sb("xn", [P, TT, DM], F32)
        stats = sb("stats", [P, TT, 6], F32)
        mean_var = sb("mean_var", [P, TT, 2], F32)
        rstd = sb("rstd", [P, TT], F32)
        minus_half = sb("minus_half", [P, TT], F32)
        xt_hi = sb("xt_hi", [P, KT, SEQ], F32R)
        xt_lo = sb("xt_lo", [P, KT, SEQ], F32R)
        qk_raw = sb("qk_raw", [P, 2, 2 * DM], F32)
        rope_b = sb("rope_b", [P, 2 * DM], F32)
        rot = sb("rot", [P, 2, TT, 2 * DM], F32)
        vals = sb("vals", [P, 2, TT, 288], F32)
        q_nat = sb("q_nat", [P, 4, TT, 2, ST], F32R)
        k_nat = sb("k_nat", [P, 2, TT, 2, ST], F32R)
        q_st = sb("q_st", [P, 2, SEQ], F32R)
        q_st2 = sb("q_st2", [P, 2, SEQ], F32R)
        k_st = sb("k_st", [P, 4, SEQ], F32R)
        row_max = sb("row_max", [P, 2, TT, 2], F32)
        masked = sb("masked", [P, 2, SEQ], BF16)
        probs = sb("probs", [P, 2 * SLOTS, SEQ], F32)
        o_t = sb("o_t", [P, SEQ], F32)
        inv_sum = sb("inv_sum", [P, TT, 4], F32)
        attn = sb("attn", [P, TT, DM], F32)
        at_hi = sb("at_hi", [P, KT, SEQ], F32R)
        at_lo = sb("at_lo", [P, KT, SEQ], F32R)
        hid = sb("hid", [P, 2, SEQ], F32)
        h_hi = sb("h_hi", [P, HT, SEQ], F32R)
        h_lo = sb("h_lo", [P, HT, SEQ], F32R)
        gate = sb("gate", [P, 2, KT, SEQ], F32)
        res = sb("res", [P, TT, DM], F32)
        square = sb("square", [P, 4], F32)
        flag_i = sb("flag_i", [P, 1], I32)
        w3_raw = rot[:, 0, :, :].rearrange("p t c -> p (t c)")[:, 0:KT * 3 * DM].rearrange("p (k c) -> p k c", k=KT)
        wo_raw = rot[:, 1, :, :].rearrange("p t c -> p (t c)")[:, 0:KT * DM].rearrange("p (k c) -> p k c", k=KT)
        w_nat = probs[:, 0:9, :].rearrange("p (w a) c -> p w (a c)", w=3)

        ps_a = [ctx.enter_context(nc.psum_tensor(f"ps_a{i}", [P, SEQ], F32)) for i in range(2)]
        ps_b = [ctx.enter_context(nc.psum_tensor(f"ps_b{i}", [P, SEQ], F32)) for i in range(B_BANKS)]
        ps_o = ctx.enter_context(nc.psum_tensor("ps_o", [P, SEQ], F32))
        ps_w = [ctx.enter_context(nc.psum_tensor(f"ps_w{i}", [P, SEQ], F32)) for i in range(WORK_BANKS)]

        const_in = sem("const_in"); w3_in = sem("w3_in"); ffn_w_in = sem("ffn_w_in"); x_in = sem("x_in")
        res_in = sem("res_in"); out_stored = sem("out_stored")
        full = {"act": sem("work_full_for_act"), "dve": sem("work_full_for_dve")}
        w3_hi_ready = sem("w3_hi_ready"); w3_ready = sem("w3_ready"); ffn_w_float = sem("ffn_w_float")
        wt_hi = sem("wt_hi"); wt_ready = sem("wt_ready"); squares_max = sem("squares_max"); all_max = sem("all_max"); flag_set = sem("flag_set")
        dve_passed = sem("dve_passed"); pool_passed = sem("pool_passed")
        zeroed = sem("zeroed"); half_set = sem("half_set")
        stats_ready = sem("stats_ready"); aggr_ready = sem("aggr_ready"); rstd_ready = sem("rstd_ready")
        xn_ready = sem("xn_ready")
        xt_hi_ready = sem("xt_hi_ready"); xt_ready = sem("xt_ready")
        qk_ready = sem("qk_ready"); v_ready = sem("v_ready"); rope_parts = sem("rope_parts"); rot_ready = sem("rot_ready")
        hi_q_ready = sem("hi_q_ready"); hi_k_ready = sem("hi_k_ready"); lo_ready = sem("lo_ready")
        q_st_ready = sem("q_st_ready"); k_st_ready = sem("k_st_ready"); q_st2_ready = sem("q_st2_ready")
        a_full = sem("a_full"); a_taken = sem("a_taken"); max_hi = sem("max_hi"); max_ready = sem("max_ready")
        b_full = sem("b_full"); exp_done = sem("exp_done"); masked_done = sem("masked_done")
        pv_done = sem("pv_done"); o_t_ready = sem("o_t_ready"); inv_ready = sem("inv_ready"); attn_ready = sem("attn_ready")
        at_hi_ready = sem("at_hi_ready"); at_ready = sem("at_ready"); prod_ready = sem("prod_ready"); res_ready = sem("res_ready")
        tanh_ready = sem("tanh_ready"); gated = sem("gated"); hid_ready = sem("hid_ready")
        h_hi_ready = sem("h_hi_ready"); h_ready = sem("h_ready"); silu_ready = sem("silu_ready")
        released = {"T2": q_st2_ready, "T1q": q_st_ready, "T1k": k_st_ready, "XT": xt_ready, "QK": qk_ready, "V": v_ready,
                    "ON": attn_ready, "AT": at_ready, "OP": prod_ready, "FT": res_ready, "G": gated, "U": hid_ready,
                    "DN": silu_ready, "WT": wt_ready}

        bank = Bank()
        MIDDLE = (BATCH - 2) // 2

        def need(eng, s, value, per_batch, it, apart=None):
            if it is not None:
                assert value > 0
                wait = eng.wait_ge(s, it * (2 * per_batch) + value)
                if apart:
                    wait.then_inc(apart, 1)
            elif value > 0:
                eng.wait_ge(s, value)

        def run(eng, do):
            for item in plan(-1) + plan(0):
                do(item, None)
            with eng.Fori(0, MIDDLE) as it:
                for item in plan(1) + plan(2):
                    do(item, it)
            for item in plan(BATCH - 1) + plan(BATCH):
                do(item, None)

        def wait_full(eng, name, item, it):
            need(eng, full[name], bank.of[item][1], bank.full_per[name], it)

        def w_of(item):
            return ps_w[bank.of[item][0]]

        def wt_cols(i):
            return P * (2 if i < 8 and i % 2 else 4)

        def wt_view(gate_up, down, i):
            if i < 8:
                w, k, half = i // 4, i // 2 % 2, i % 2
                return gate_up[:, w, k, half * 512:half * 512 + wt_cols(i)]
            return down[:, 2 * (i - 8):2 * (i - 8) + 2, :].rearrange("p j d -> p (j d)")

        def tanh_at(b, j):
            return b * (HT + KT) + j + 1

        def rot_of(b, pair, which):
            c = which * DM + pair * 2 * HD
            return rot[:, b % 2, :, c:c + 2 * HD].rearrange("p t (h c) -> p t h c", h=2)

        def rotate(eng, tensor_tensor, item, it):
            kind, b, i = item
            t, part = divmod(i, 4)
            src, dst = qk_raw[:, t % 2, :], rot[:, b % 2, t, :]
            by_head = lambda ap: ap.rearrange("p (h c) -> p h c", c=HD)
            by_two = lambda ap: ap.rearrange("p (h j e) -> p h j e", j=HD // 2, e=2)
            cos = cst[:, C_COS + t * HD:C_COS + (t + 1) * HD].rearrange("p (a c) -> p a c", a=1).broadcast_to([P, 2 * HEADS, HD])
            sin = cst[:, C_SIN + t * HD:C_SIN + (t + 1) * HD].rearrange("p (a j e) -> p a j e", a=1, e=2)\
                .broadcast_to([P, 2 * HEADS, HD // 2, 2])
            if part == 0:
                need(eng, qk_ready, b * TT + t + 1, TT, it)
                tensor_tensor(by_head(dst), by_head(src), cos, ALU.mult).then_inc(rope_parts, 1)
            elif part < 3:
                e = part - 1
                if e == 0:
                    need(eng, rot_ready, b * TT + t, TT, it)
                tensor_tensor(by_two(rope_b[:])[:, :, :, e], by_two(src)[:, :, :, 1 - e], sin[:, :, :, e],
                              ALU.mult).then_inc(rope_parts, 1)
            else:
                need(eng, rope_parts, 3 * (b * TT + t + 1), 3 * TT, it)
                tensor_tensor(dst, dst, rope_b[:], ALU.add).then_inc(rot_ready, 1)

        def high_parts(name, eng, copy, passed, item, it):
            kind, b, i = item
            if HI_ENGINE[kind] != name:
                return
            n = b * PAIRS + i
            need(eng, rot_ready, (b + 1) * TT, TT, it)
            if kind == "HIq":
                need(eng, q_st2_ready, n - 3, PAIRS, it, apart=passed)
            else:
                need(eng, k_st_ready, n - 1, PAIRS, it, apart=passed)
            nat, which, places, ready = (q_nat[:, i % 4], 0, (0, 1), hi_q_ready) if kind == "HIq" else (k_nat[:, i % 2], 1, (0, 2), hi_k_ready)
            for at in places:
                copy(nat[:, :, :, at * HD:(at + 1) * HD], rot_of(b, i, which)).then_inc(ready, 1)

        CONST_LOADS = 1 + 3 + KT
        block = ctx.enter_context(nc.Block())

        @block.sync
        def _(sp):
            by_tile = lambda ap: ap.rearrange("(t p) d -> p t d", p=P)
            sp.dma_start(xn[:], by_tile(x[0])).then_inc(x_in, 16)
            sp.dma_start(cst[:], consts).then_inc(const_in, 16)
            for j, v in enumerate((bq, bk, bv)):
                sp.dma_start(bias3[:, j * DM:(j + 1) * DM],
                             v.rearrange("(a d) -> a d", a=1).broadcast_to([P, DM])).then_inc(const_in, 16)
            for k in range(KT):
                sp.dma_start(bo_col[:, k:k + 1], bo[k * P:(k + 1) * P].rearrange("(p a) -> p a", a=1)).then_inc(const_in, 16)
            for j, w in enumerate((wq, wk, wv)):
                sp.dma_start(w3_raw[:, :, j * DM:(j + 1) * DM], by_tile(w)).then_inc(w3_in, 16)
            sp.dma_start(wo_raw, by_tile(wo)).then_inc(w3_in, 16)
            for j, w in enumerate((w_gate, w_up)):
                sp.dma_start(w_nat[:, j, :].bitcast(I32).rearrange("p (t d) -> p t d", d=DM), by_tile(w)).then_inc(ffn_w_in, 16)
            sp.dma_start(w_nat[:, 2, :].bitcast(I32).rearrange("p (t d) -> p t d", d=HID), by_tile(w_down)).then_inc(ffn_w_in, 16)
            sp.dma_start(res[:], by_tile(x[0])).then_inc(res_in, 16)
            sp.wait_ge(xt_ready, KT)
            sp.dma_start(xn[:], by_tile(x[1])).then_inc(x_in, 16)
            with sp.Fori(1, BATCH - 1) as b:
                sp.wait_ge(xt_ready, b * KT + KT)
                sp.dma_start(xn[:], x[bass.ds(b + 1, 1), :, :].rearrange("a (t p) d -> p (a t) d", p=P)).then_inc(x_in, 16)
                sp.wait_ge(res_ready, b * 2)
                sp.dma_start(out[bass.ds(b - 1, 1), :, :].rearrange("a (t p) d -> p (a t) d", p=P), res[:]).then_inc(out_stored, 16)
                sp.wait_ge(out_stored, b * 16)
                sp.dma_start(res[:], x[bass.ds(b, 1), :, :].rearrange("a (t p) d -> p (a t) d", p=P)).then_inc(res_in, 16)
            for b in (BATCH - 2, BATCH - 1):
                sp.wait_ge(res_ready, (b + 1) * 2)
                sp.dma_start(by_tile(out[b]), res[:]).then_inc(out_stored, 16)
                sp.wait_ge(out_stored, (b + 1) * 16)
                if b + 1 < BATCH:
                    sp.dma_start(res[:], by_tile(x[b + 1])).then_inc(res_in, 16)

        @block.tensor
        def _(pe):
            flag = {}

            def take_bank(item, it):
                before = bank.of[item][2]
                if before:
                    need(pe, released[before[0]], before[1], bank.kind_per[before[0]], it)
                return w_of(item)

            def done(ins, item):
                ins.then_inc(full[WORK[item[0]][0]], 1)

            def group(dst, terms, middle=()):
                for i, (w, m) in enumerate(terms):
                    if middle and i == 1:
                        with pe.If(flag["has_lo"] > 0):
                            for wl, ml in middle:
                                pe.matmul(dst, wl, ml, start=False, stop=False)
                    last = pe.matmul(dst, w, m, start=(i == 0), stop=(i == len(terms) - 1))
                return last

            def do(item, it):
                kind, b, i = item
                n = b * PAIRS + i
                if kind == "WQ":
                    pe.wait_ge(const_in, 16 * CONST_LOADS)
                    pe.wait_ge(zeroed, 5)
                elif kind == "XT":
                    need(pe, xn_ready, (b + 1) * TT, TT, it)
                    dst = take_bank(item, it)
                    for tt in range(TT):
                        last = pe.transpose(dst[:, tt * P:(tt + 1) * P], xn[:, tt, i * P:(i + 1) * P], ident)
                    done(last, item)
                elif kind in ("QK", "V"):
                    if i == 0:
                        need(pe, xt_ready, (b + 1) * KT, KT, it)
                        if b == 0:
                            pe.wait_ge(w3_ready, 2)
                    dst = take_bank(item, it)
                    c0, c1 = (0, 2 * DM) if kind == "QK" else (2 * DM, 3 * DM)
                    tok = slice(i * P, (i + 1) * P)
                    terms = []
                    for k in range(KT):
                        terms += [(xt_hi[:, k, tok], w3_hi[:, k, c0:c1]), (xt_hi[:, k, tok], w3_lo[:, k, c0:c1]),
                                  (xt_lo[:, k, tok], w3_hi[:, k, c0:c1])]
                    done(group(dst[:, 0:c1 - c0], terms), item)
                elif kind == "WT":
                    if i == 0:
                        pe.wait_ge(ffn_w_float, 3)
                    dst = take_bank(item, it)
                    if i < 8:
                        w, k, half = i // 4, i // 2 % 2, i % 2
                        for a, t in enumerate(range(4 * half, min(4 * half + 4, HT))):
                            last = pe.transpose(dst[:, a * P:(a + 1) * P], w_nat[:, w, t * DM + k * P:t * DM + (k + 1) * P], ident)
                    else:
                        for a, (j, m) in enumerate([(2 * (i - 8) + jj, m) for jj in range(2) for m in range(KT)]):
                            last = pe.transpose(dst[:, a * P:(a + 1) * P], w_nat[:, 2, m * HID + j * P:m * HID + (j + 1) * P], ident)
                    done(last, item)
                elif kind == "FLAG":
                    pe.wait_ge(flag_set, 1)
                    flag["has_lo"] = pe.value_load(flag_i[0:1, 0:1], min_val=0, max_val=1)
                elif kind in ("T1q", "T1k"):
                    if kind == "T1q":
                        need(pe, lo_ready, 2 * (n + 1), 2 * PAIRS, it)
                    dst = take_bank(item, it)
                    for tt in range(TT):
                        src = (q_nat[:, i % 4, tt] if kind == "T1q" else k_nat[:, i % 2, tt]).rearrange("p h c -> p (h c)")
                        last = pe.transpose(dst[:, tt * P:(tt + 1) * P].bitcast(F32R), src, ident_r[:])
                    done(last, item)
                elif kind == "T2":
                    need(pe, max_ready, n + 1, PAIRS, it)
                    dst = take_bank(item, it)
                    for tt in range(TT):
                        last = pe.transpose(dst[:, tt * P:(tt + 1) * P].bitcast(F32R), q_nat[:, i % 4, tt].rearrange("p h c -> p (h c)"), ident_r[:])
                    done(last, item)
                elif kind == "A":
                    pair, c = divmod(i, CHUNKS)
                    m = b * PAIRS * CHUNKS + i
                    if c == 0:
                        need(pe, q_st_ready, b * PAIRS + pair + 1, PAIRS, it)
                        need(pe, k_st_ready, b * PAIRS + pair + 1, PAIRS, it)
                    need(pe, a_taken, m - 1, PAIRS * CHUNKS, it)
                    for h, qt, col in A_PARTS[c]:
                        rows = slice(h * ST, h * ST + 3 * HD)
                        w = (qt + 1) * P
                        last = pe.matmul(ps_a[i % 2][:, col:col + w], q_st[rows, pair % 2, qt * P:(qt + 1) * P],
                                         k_st[rows, pair % 4, 0:w], start=True, stop=True)
                    last.then_inc(a_full, 1)
                elif kind == "B":
                    pair, c = divmod(i, CHUNKS)
                    if c == 0:
                        need(pe, q_st2_ready, b * PAIRS + pair + 1, PAIRS, it)
                    per = PAIRS * CHUNKS
                    need(pe, exp_done, b * per + i + 1 - B_BANKS, per, it)
                    for h, kt, col in B_PARTS[c]:
                        rows = slice(h * ST, (h + 1) * ST)
                        w = SEQ - kt * P
                        last = pe.matmul(ps_b[i % B_BANKS][:, col:col + w], k_st[rows, pair % 4, kt * P:(kt + 1) * P],
                                         q_st2[rows, pair % 2, kt * P:SEQ], start=True, stop=True)
                    last.then_inc(b_full, 1)
                elif kind == "PV":
                    group_, step = divmod(i, TT)
                    g, kt = b * GROUPS + group_, PV_ORDER[step]
                    if step == 0:
                        need(pe, o_t_ready, g, GROUPS, it)
                        need(pe, v_ready, (b + 1) * TT, TT, it)
                    if step != 2:
                        need(pe, masked_done, CHUNKS * (2 * g + 1) + (2, 4, 0, 6)[step], PAIRS * CHUNKS, it)
                    for hh in range(4):
                        slot, col = P_AT[kt][hh % 2]
                        head = 4 * group_ + hh
                        last = pe.matmul(ps_o[32 * hh:32 * hh + 32, kt * P:SEQ],
                                         vals[:, b % 2, kt, head * VW:head * VW + 32],
                                         probs[:, (hh // 2) * SLOTS + slot, col:col + SEQ - kt * P],
                                         start=(step == 0), stop=(step == TT - 1), skip_group_check=True)
                    last.then_inc(pv_done, 1)
                elif kind == "ON":
                    need(pe, o_t_ready, b * GROUPS + i + 1, GROUPS, it)
                    dst = take_bank(item, it)
                    for tt in range(TT):
                        last = pe.transpose(dst[:, tt * P:(tt + 1) * P], o_t[:, tt * P:(tt + 1) * P], ident)
                    done(last, item)
                elif kind == "AT":
                    need(pe, attn_ready, (b + 1) * GROUPS, GROUPS, it)
                    dst = take_bank(item, it)
                    for tt in range(TT):
                        last = pe.transpose(dst[:, tt * P:(tt + 1) * P], attn[:, tt, i * P:(i + 1) * P], ident)
                    done(last, item)
                elif kind == "OP":
                    need(pe, at_ready, (b + 1) * KT, KT, it)
                    dst = take_bank(item, it)
                    col = slice(i * P, (i + 1) * P)
                    terms = []
                    for k in range(KT):
                        terms += [(wo_hi[:, k, col], at_hi[:, k, :]), (wo_lo[:, k, col], at_hi[:, k, :]),
                                  (wo_hi[:, k, col], at_lo[:, k, :])]
                    done(group(dst[:, :], terms), item)
                elif kind == "FT":
                    need(pe, prod_ready, (b + 1) * KT, KT, it)
                    dst = take_bank(item, it)
                    for a, (tt, m) in enumerate([(2 * i + t, m) for t in range(2) for m in range(KT)]):
                        last = pe.transpose(dst[:, a * P:(a + 1) * P], hid[:, m, tt * P:(tt + 1) * P], ident)
                    done(last, item)
                elif kind in ("G", "U"):
                    if kind == "G" and i == 0:
                        need(pe, xt_ready, (b + 1) * KT, KT, it)
                    dst = take_bank(item, it)
                    w, col = (0 if kind == "G" else 1), slice(i * P, (i + 1) * P)
                    terms = [(wgu_hi[:, w, k, col], xt[:, k, :]) for k in range(KT) for xt in (xt_hi, xt_lo)]
                    low = [(wgu_lo[:, w, k, col], xt_hi[:, k, :]) for k in range(KT)]
                    done(group(dst[:, :], terms, low), item)
                elif kind == "DN":
                    need(pe, h_ready, (b + 1) * HT, HT, it)
                    dst = take_bank(item, it)
                    col = slice(i * P, (i + 1) * P)
                    terms = [(wd_hi[:, j, col], h[:, j, :]) for j in range(HT) for h in (h_hi, h_lo)]
                    low = [(wd_lo[:, j, col], h_hi[:, j, :]) for j in range(HT)]
                    done(group(dst[:, :], terms, low), item)

            run(pe, do)

        @block.scalar
        def _(act):
            def do(item, it):
                kind, b, i = item
                n = b * PAIRS + i
                if kind == "WQ":
                    act.wait_ge(w3_in, 64)
                    nc.scalar.copy(w3_hi[:], w3_raw).then_inc(w3_hi_ready, 1)
                    nc.scalar.copy(wo_hi[:], wo_raw).then_inc(w3_hi_ready, 1)
                elif kind == "WC":
                    act.wait_ge(ffn_w_in, 48)
                    for w in range(3):
                        nc.scalar.copy(w_nat[:, w, :], w_nat[:, w, :].bitcast(I32)).then_inc(ffn_w_float, 1)
                elif kind == "XT":
                    wait_full(act, "act", item, it)
                    nc.scalar.copy(xt_hi[:, i, :], w_of(item)[:, :]).then_inc(xt_hi_ready, 1)
                elif kind == "WT":
                    wait_full(act, "act", item, it)
                    nc.scalar.copy(wt_view(wgu_hi, wd_hi, i), w_of(item)[:, 0:wt_cols(i)]).then_inc(wt_hi, 1)
                elif kind in ("T1q", "T1k", "T2"):
                    wait_full(act, "act", item, it)
                    dst, ready = {"T1q": (q_st[:, i % 2, :], q_st_ready), "T1k": (k_st[:, i % 4, :], k_st_ready),
                                  "T2": (q_st2[:, i % 2, :], q_st2_ready)}[kind]
                    nc.scalar.copy(dst, w_of(item)[:, :]).then_inc(ready, 1)
                elif kind in ("HIq", "HIk"):
                    high_parts("act", act, nc.scalar.copy, None, item, it)
                elif kind == "B":
                    pair, c = divmod(i, CHUNKS)
                    m = b * PAIRS * CHUNKS + i
                    need(act, b_full, m + 1, PAIRS * CHUNKS, it)
                    if pair % 2 == 0:
                        need(act, pv_done, TT * ((b * PAIRS + pair) // 2 - 1) + (1, 1, 3, 3, 4, 4)[c], TT * GROUPS, it)
                    slot, col = slot_of(c)
                    nc.scalar.activation(probs[:, (pair % 2) * SLOTS + slot, col:col + WIDTH[c]], ps_b[i % B_BANKS][:, 0:WIDTH[c]], ACT.Exp,
                                         scale=QSCALE).then_inc(exp_done, 1)
                elif kind == "PV" and i % TT == TT - 1:
                    need(act, pv_done, b * GROUPS * TT + i + 1, GROUPS * TT, it)
                    nc.scalar.copy(o_t[:, :], ps_o[:, :]).then_inc(o_t_ready, 1)
                elif kind == "AT":
                    wait_full(act, "act", item, it)
                    nc.scalar.copy(at_hi[:, i, :], w_of(item)[:, :]).then_inc(at_hi_ready, 1)
                elif kind == "G":
                    wait_full(act, "act", item, it)
                    if i >= 2:
                        need(act, h_ready, b * HT + i - 1, HT, it)
                    elif b:
                        need(act, silu_ready, b * KT, KT, it)
                    nc.scalar.activation(hid[:, i % 2, :], w_of(item)[:, :], ACT.Tanh,
                                         scale=0.5 * WSCALE).then_inc(tanh_ready, 1)
                elif kind == "HL":
                    need(act, hid_ready, b * HT + i + 1, HT, it)
                    nc.scalar.copy(h_hi[:, i, :], hid[:, i % 2, :]).then_inc(h_hi_ready, 1)
                elif kind == "DN":
                    wait_full(act, "act", item, it)
                    nc.scalar.activation(hid[:, i, :], w_of(item)[:, :], ACT.Tanh,
                                         scale=0.5 * WSCALE).then_inc(tanh_ready, 1)

            run(act, do)

        @block.vector
        def _(dve):
            def do(item, it):
                kind, b, i = item
                n = b * PAIRS + i
                if kind == "WQ":
                    nc.vector.memset(q_nat[:].bitcast(F32), 0.0).then_inc(zeroed, 1)
                    nc.vector.memset(k_nat[:].bitcast(F32), 1.0).then_inc(zeroed, 1)
                    nc.vector.memset(vals[:], 1.0).then_inc(zeroed, 1)
                    nc.vector.memset(square[:], 0.0).then_inc(zeroed, 1)
                    dve.wait_ge(const_in, 16 * CONST_LOADS)
                    nc.vector.tensor_copy(ident_r[:], ident).then_inc(zeroed, 1)
                    dve.wait_ge(zeroed, 5)
                elif kind == "WC":
                    dve.wait_ge(w3_hi_ready, 2)
                    nc.vector.tensor_tensor(w3_lo[:], w3_raw, w3_hi[:].bitcast(F32), ALU.subtract).then_inc(w3_ready, 1)
                    nc.vector.tensor_tensor(wo_lo[:], wo_raw, wo_hi[:].bitcast(F32), ALU.subtract).then_inc(w3_ready, 1)
                elif kind == "FLAG":
                    dve.wait_ge(ffn_w_float, 3)
                    for w in range(3):
                        if w:
                            dve.wait_ge(squares_max, w)
                        nc.vector.tensor_tensor_reduce(out=h_lo[:, 0:3, :].rearrange("p j c -> p (j c)"),
                                                       in0=w_nat[:, w, :], in1=w_nat[:, w, :], scale=1.0, scalar=0.0,
                                                       op0=ALU.mult, op1=ALU.max, accum_out=square[:, w:w + 1])\
                            .then_inc(squares_max, 1)
                    dve.wait_ge(squares_max, 3)
                    nc.vector.tensor_reduce(square[:, 3:4], square[:, 0:3], AX.X, ALU.max).then_inc(squares_max, 1)
                    dve.wait_ge(all_max, 1)
                    nc.vector.tensor_scalar(flag_i[:], square[:, 0:1], float(1 << 24), None, ALU.is_gt).then_inc(flag_set, 1)
                elif kind == "ST":
                    need(dve, x_in, 16 * (b + 1), 16, it)
                    need(dve, aggr_ready, TT * b, TT, it)
                    for tt in range(TT):
                        nc.vector.bn_stats(stats[:, tt, :], xn[:, tt, :]).then_inc(stats_ready, 1)
                    need(dve, stats_ready, TT * (b + 1), TT, it, apart=dve_passed)
                    for tt in range(TT):
                        nc.vector.bn_aggr(mean_var[:, tt, :], stats[:, tt, :]).then_inc(aggr_ready, 1)
                elif kind == "XT":
                    need(dve, xt_hi_ready, b * KT + i + 1, KT, it)
                    nc.vector.tensor_tensor(xt_lo[:, i, :], w_of(item)[:, :], xt_hi[:, i, :].bitcast(F32), ALU.subtract)\
                        .then_inc(xt_ready, 1)
                elif kind == "QK":
                    wait_full(dve, "dve", item, it)
                    need(dve, rot_ready, b * TT + i - 1, TT, it)
                    nc.vector.tensor_tensor(qk_raw[:, i % 2, :], w_of(item)[:, :], bias3[:, 0:2 * DM], ALU.add)\
                        .then_inc(qk_ready, 1)
                elif kind == "V":
                    wait_full(dve, "dve", item, it)
                    v3 = vals[:, b % 2, i, 0:HEADS * VW].rearrange("p (h c) -> p h c", c=VW)[:, :, 0:HD]
                    nc.vector.tensor_tensor(v3, w_of(item)[:, 0:DM].rearrange("p (h c) -> p h c", c=HD),
                                            bias3[:, 2 * DM:3 * DM].rearrange("p (h c) -> p h c", c=HD), ALU.add)\
                        .then_inc(v_ready, 1)
                elif kind == "WT":
                    dve.wait_ge(wt_hi, i + 1)
                    hi, lo = wt_view(wgu_hi, wd_hi, i), wt_view(wgu_lo, wd_lo, i)
                    nc.vector.tensor_tensor(lo, w_of(item)[:, 0:wt_cols(i)], hi.bitcast(F32), ALU.subtract)\
                        .then_inc(wt_ready, 1)
                elif kind == "ROPE" and b == 0:
                    rotate(dve, nc.vector.tensor_tensor, item, it)
                elif kind in ("HIq", "HIk"):
                    high_parts("dve", dve, nc.vector.tensor_copy, dve_passed, item, it)
                elif kind == "LOq":
                    need(dve, hi_q_ready, 2 * (n + 1), 2 * PAIRS, it)
                    qn = q_nat[:, i % 4, :, :, :]
                    nc.vector.tensor_tensor(qn[:, :, :, 2 * HD:3 * HD], rot_of(b, i, 0), qn[:, :, :, 0:HD].bitcast(F32), ALU.subtract)\
                        .then_inc(lo_ready, 1)
                elif kind == "LOk":
                    need(dve, hi_k_ready, 2 * (n + 1), 2 * PAIRS, it)
                    kn = k_nat[:, i % 2, :, :, :]
                    nc.vector.tensor_tensor(kn[:, :, :, HD:2 * HD], rot_of(b, i, 1), kn[:, :, :, 0:HD].bitcast(F32), ALU.subtract)\
                        .then_inc(lo_ready, 1)
                elif kind == "A":
                    pair, c = divmod(i, CHUNKS)
                    m = b * PAIRS * CHUNKS + i
                    if c == 0:
                        need(dve, max_ready, b * PAIRS + pair - 1, PAIRS, it)
                    need(dve, a_taken, m - 1, PAIRS * CHUNKS, it)
                    need(dve, a_full, m + 1, PAIRS * CHUNKS, it, apart=dve_passed)
                    for h, qt, col in A_PARTS[c]:
                        w = (qt + 1) * P
                        last = nc.vector.tensor_tensor_reduce(
                            out=masked[:, i % 2, col:col + w], in0=ps_a[i % 2][:, col:col + w], in1=cst[:, C_MASK + SEQ - w:C_MASK + SEQ],
                            scale=1.0, scalar=-3e38, op0=ALU.add, op1=ALU.max, accum_out=row_max[:, pair % 2, qt, h:h + 1])
                    last.then_inc(a_taken, 1)
                elif kind == "MX":
                    need(dve, a_taken, (n + 1) * CHUNKS, PAIRS * CHUNKS, it)
                    mx, qn = row_max[:, i % 2, :, :], q_nat[:, i % 4, :, :, :]
                    nc.vector.tensor_scalar(qn[:, :, :, 3 * HD], mx, -1.0, None, ALU.mult).then_inc(max_hi, 1)
                    need(dve, max_hi, n + 1, PAIRS, it)
                    nc.vector.scalar_tensor_tensor(out=qn[:, :, :, 3 * HD + 1], in0=mx, scalar=-1.0, in1=qn[:, :, :, 3 * HD].bitcast(F32),
                                                   op0=ALU.mult, op1=ALU.subtract).then_inc(max_ready, 1)
                elif kind == "ON":
                    wait_full(dve, "dve", item, it)
                    o4 = w_of(item)[:, :].rearrange("p (t h c) -> p t h c", t=TT, h=4)
                    g = b * GROUPS + i
                    need(dve, attn_ready, g, GROUPS, it)
                    nc.vector.reciprocal(inv_sum[:], o4[:, :, :, HD]).then_inc(inv_ready, 1)
                    need(dve, inv_ready, g + 1, GROUPS, it)
                    nc.vector.tensor_tensor(attn[:, :, i * 64:(i + 1) * 64].rearrange("p t (h c) -> p t h c", h=4),
                                            o4[:, :, :, 0:HD], inv_sum[:].rearrange("p t (h a) -> p t h a", a=1)
                                            .broadcast_to([P, TT, 4, HD]), ALU.mult).then_inc(attn_ready, 1)
                elif kind == "AT":
                    need(dve, at_hi_ready, b * KT + i + 1, KT, it)
                    nc.vector.tensor_tensor(at_lo[:, i, :], w_of(item)[:, :], at_hi[:, i, :].bitcast(F32), ALU.subtract)\
                        .then_inc(at_ready, 1)
                elif kind == "OP":
                    wait_full(dve, "dve", item, it)
                    nc.vector.scalar_tensor_tensor(out=hid[:, i, :], in0=w_of(item)[:, :], scalar=bo_col[:, i:i + 1],
                                                   in1=gate[:, b % 2, i, :], op0=ALU.add, op1=ALU.mult).then_inc(prod_ready, 1)
                elif kind == "FT":
                    wait_full(dve, "dve", item, it)
                    if i == 0:
                        need(dve, res_in, 16 * (b + 1), 16, it)
                    r = res[:, 2 * i:2 * i + 2, :].rearrange("p t d -> p (t d)")
                    nc.vector.scalar_tensor_tensor(out=r, in0=w_of(item)[:, :], scalar=0.5 * WSCALE, in1=r,
                                                   op0=ALU.mult, op1=ALU.add).then_inc(res_ready, 1)
                elif kind == "G":
                    need(dve, tanh_ready, tanh_at(b, i), HT + KT, it)
                    nc.vector.scalar_tensor_tensor(out=hid[:, i % 2, :], in0=hid[:, i % 2, :], scalar=1.0,
                                                   in1=w_of(item)[:, :], op0=ALU.add, op1=ALU.mult).then_inc(gated, 1)
                elif kind == "U":
                    wait_full(dve, "dve", item, it)
                    need(dve, gated, b * HT + i + 1, HT, it)
                    nc.vector.scalar_tensor_tensor(out=hid[:, i % 2, :], in0=w_of(item)[:, :], scalar=0.5 * WSCALE * WSCALE,
                                                   in1=hid[:, i % 2, :], op0=ALU.mult, op1=ALU.mult).then_inc(hid_ready, 1)
                elif kind == "HL":
                    need(dve, h_hi_ready, b * HT + i + 1, HT, it)
                    nc.vector.tensor_tensor(h_lo[:, i, :], hid[:, i % 2, :], h_hi[:, i, :].bitcast(F32), ALU.subtract)\
                        .then_inc(h_ready, 1)
                elif kind == "DN":
                    need(dve, tanh_ready, tanh_at(b, HT + i), HT + KT, it)
                    nc.vector.scalar_tensor_tensor(out=gate[:, b % 2, i, :], in0=hid[:, i, :], scalar=1.0,
                                                   in1=w_of(item)[:, :], op0=ALU.add, op1=ALU.mult).then_inc(silu_ready, 1)

            run(dve, do)

        @block.gpsimd
        def _(pool):
            def do(item, it):
                kind, b, i = item
                n = b * PAIRS + i
                if kind == "WQ":
                    pool.wait_ge(const_in, 16 * CONST_LOADS)
                    nc.gpsimd.memset(minus_half[:], -0.5).then_inc(half_set, 1)
                    pool.wait_ge(half_set, 1)
                    pool.wait_ge(zeroed, 5)
                elif kind == "RS":
                    need(pool, xn_ready, TT * b, TT, it)
                    need(pool, aggr_ready, TT * (b + 1), TT, it, apart=pool_passed)
                    nc.gpsimd.tensor_scalar(rstd[:], mean_var[:, :, 1], EPS, None, ALU.add).then_inc(rstd_ready, 1)
                    need(pool, rstd_ready, 2 * b + 1, 2, it)
                    nc.gpsimd.tensor_tensor(rstd[:], rstd[:], minus_half[:], ALU.pow).then_inc(rstd_ready, 1)
                elif kind == "NM":
                    if i == 0:
                        need(pool, rstd_ready, 2 * b + 2, 2, it, apart=pool_passed)
                    nc.gpsimd.tensor_scalar(xn[:, i, :], xn[:, i, :], mean_var[:, i, 0:1], rstd[:, i:i + 1],
                                            ALU.subtract, ALU.mult).then_inc(xn_ready, 1)
                elif kind == "ROPE" and b > 0:
                    rotate(pool, nc.gpsimd.tensor_tensor, item, it)
                elif kind in ("HIq", "HIk"):
                    high_parts("pool", pool, nc.gpsimd.tensor_copy, pool_passed, item, it)
                elif kind == "B":
                    pair, c = divmod(i, CHUNKS)
                    m = b * PAIRS * CHUNKS + i
                    need(pool, exp_done, m + 1, PAIRS * CHUNKS, it, apart=pool_passed)
                    blocks = [col for _, _, col in B_PARTS[c]]
                    slot, col = slot_of(c)
                    pr = probs[:, (pair % 2) * SLOTS + slot, col:col + WIDTH[c]]
                    if len(blocks) == 1:
                        v, pattern = pr[:, 0:P], [[1, P]]
                    else:
                        a = pr[:, 0:P]
                        ap = list(a.ap)
                        v = bass.AP(tensor=a.tensor, offset=a.offset, ap=[list(ap[0]), [blocks[1], 2], [1, P]])
                        pattern = [[0, 2], [1, P]]
                    nc.gpsimd.affine_select(out=v, in_=v, compare_op=ALU.is_ge, fill=0.0, base=0, pattern=pattern,
                                            channel_multiplier=-1).then_inc(masked_done, 1)
                elif kind == "FLAG":
                    pool.wait_ge(squares_max, 4)
                    nc.gpsimd.partition_all_reduce(square[:, 0:1], square[:, 3:4], P, bass.bass_isa.ReduceOp.max).then_inc(all_max, 1)

            run(pool, do)


_INS = ["L0_attn_x", "L0_attn_wq", "L0_attn_bq", "L0_attn_wk", "L0_attn_bk", "L0_attn_wv", "L0_attn_bv", "L0_attn_wo",
        "L0_attn_bo", "L0_ffn_w_gate", "L0_ffn_w_up", "L0_ffn_w_down"]


def kernel(**inputs):
    import concourse.bacc as bacc
    from concourse.bass_utils import run_bass_kernel_spmd

    nc = bacc.Bacc("TRN2", target_bir_lowering=False, num_devices=1)
    arrays = {name: np.ascontiguousarray(inputs[name]) for name in _INS}
    arrays["shape_constants"] = shape_constants()
    args = [nc.dram_tensor(name, a.shape, mybir.dt.from_np(a.dtype), kind="ExternalInput").ap()
            for name, a in arrays.items()]
    result = nc.dram_tensor("result", (BATCH, SEQ, DM), F32, kind="ExternalOutput").ap()
    build(nc, *args, result)
    r = run_bass_kernel_spmd(nc, [arrays], core_ids=[0])
    return r.results[0]["result"]
```

```python
from contextlib import ExitStack

import numpy as np

import concourse.bass as bass
from concourse import mybir

ALU = mybir.AluOpType
ACT = mybir.ActivationFunctionType
AX = mybir.AxisListType
F32 = mybir.dt.float32
F32R = mybir.dt.float32r
I32 = mybir.dt.int32
BF16 = mybir.dt.bfloat16

P = 128
BATCH, SEQ, DM = 8, 512, 256
HEADS, HD = 16, 16
HID = 768
TT = SEQ // P
KT = DM // P
HT = HID // P
PAIRS = HEADS // 2
GROUPS = HEADS // 4
ST = 4 * HD
VW = HD + 1
CHUNKS = 6
SLOTS = 5
DVE_ROTATES = 2
WORK_BANKS = 7
HI_ENGINE = {"HIq": "act", "HIk": "pool"}
QSCALE = float(HD) ** -0.5
WSCALE = 1.0 / 127.0
EPS = 1e-5
NEG = -1e9 / QSCALE

C_ID, C_MASK, C_COS, C_SIN = 0, P, P + SEQ, P + SEQ + TT * HD
C_ALL = C_SIN + TT * HD


def shape_constants():
    inv_freq = (np.float32(1.0) / np.float32(10000.0) ** (np.arange(0, HD, 2, dtype=np.float32) / np.float32(HD)))
    freqs = np.arange(SEQ, dtype=np.float32)[:, None] * inv_freq.astype(np.float32)[None, :]
    cos, sin = np.cos(freqs), np.sin(freqs)
    cos2 = np.repeat(cos, 2, axis=1)
    sin2 = np.stack([-sin, sin], axis=-1).reshape(SEQ, HD)
    by_tile = lambda t: t.reshape(TT, P, HD).transpose(1, 0, 2).reshape(P, TT * HD)
    mask = np.zeros((P, SEQ), np.float32)
    mask[:, SEQ - P:] = np.where(np.arange(P)[None, :] > np.arange(P)[:, None], NEG, 0.0)
    return np.concatenate([np.eye(P, dtype=np.float32), mask, by_tile(cos2), by_tile(sin2)], axis=1).astype(np.float32)


B_PARTS = [[(h, kt, col) for kt, col in part] for part in ([(0, 0)], [(1, 0), (3, 384)], [(2, 0)]) for h in range(2)]
A_PARTS = [[(h, TT - 1 - kt, col) for h, kt, col in part] for part in B_PARTS]
WIDTH = [SEQ, SEQ, SEQ, SEQ, SEQ // 2, SEQ // 2]


def slot_of(c):
    return (c, 0) if c < 4 else (4, (c - 4) * (SEQ // 2))


P_AT = [[next((slot_of(c)[0], slot_of(c)[1] + col) for c, parts in enumerate(B_PARTS) for hh, k, col in parts
              if (hh, k) == (h, kt)) for h in range(2)] for kt in range(TT)]
PV_ORDER = [0, 1, 3, 2]

WORK = {"A": ("dve", "a_taken"), "B": ("act", "exp_done"), "T2": ("act", "q_st2_ready"),
        "T1q": ("act", "q_st_ready"), "T1k": ("act", "k_st_ready"),
        "XT": ("act", "xt_ready"), "QK": ("dve", "qk_ready"), "V": ("dve", "v_ready"), "ON": ("dve", "attn_ready"),
        "AT": ("act", "at_ready"), "OP": ("dve", "sum_ready"), "G": ("act", "gated"),
        "U": ("dve", "hid_ready"), "DN": ("act", "silu_ready"), "WT": ("act", "wt_ready")}
WT_USES = 11


AHEAD = {"B": -1, "T2": 0, "A": 1, "MX": 1, "T1q": 2, "T1k": 2, "HIq": 3, "HIk": 3, "LOq": 3, "LOk": 3}

START = {
    "pe": """
        WQ XT:0 XT:1 WC V:0 QK:0 V:1 WT:0 QK:1 WT:1 WT:2 QK:2 WT:3 WT:4 V:2 WT:5 WT:6 V:3 QK:3 WT:7 WT:8 WT:9 WT:10 FLAG
        U:0 G:0 G:1 T1q:0 U:1 T1k:0 A:0 A:1 T1k:1 A:2 A:3 A:4 A:5 T1q:1
    """,
    "act": """
        WQ XT:0 XT:1 WC WT:0 WT:1 WT:2 WT:3 WT:4 WT:5 WT:6 WT:7 WT:8 WT:9 WT:10 G:0 HIq:0 G:1 HIq:1 T1q:0 HIq:2 HL:0
        T1k:0 T1k:1 T1q:1
    """,
    "dve": """
        WQ ST:0 NM:0 NM:1 NM:2 NM:3 XT:0 XT:1 WC V:0 QK:0 ROPE:0 ROPE:1 V:1 ROPE:2 SQ WT:0 ROPE:3 QK:1 ROPE:4 ROPE:5
        WT:1 WT:2 QK:2 ROPE:6 ROPE:7 WT:3 WT:4 V:2 WT:5 V:3 WT:6 WT:7 QK:3 WT:8 FLAG WT:9 WT:10 G:0 LOq:0 U:0 LOk:0 G:1
        U:1 HL:0 LOk:1 LOq:1 A:0 A:1 A:2 LOq:2 A:3 A:4 A:5 MX:0 LOk:2
    """,
    "pool": """
        WQ RS:0 WC SQ ROPE:8 ROPE:9 ROPE:10 ROPE:11 ROPE:12 ROPE:13 ROPE:14 ROPE:15 HIk:0 HIk:1 HIk:2
    """,
}
SCHEDULE = {
    "pe": """
        G:2 B:0 B:1 A:0 ON:2< A:1 U:2 B:2 T1q B:3 G:3 A:2 A:3 T1k U:3 PV:12< A:4 B:4 B:5 G:4 T2 A:5 U:4 PV:13< PV:14<
        B:0 A:0 A:1 B:1 G:5 U:5 T1q A:2 B:2 PV:15< B:3 B:4 T1k A:3 T2 A:4 XT:0> XT:1> A:5 B:5
        DN:0 V:0> B:0 A:0 B:1 A:1 QK:0> B:2 V:1> A:2 B:3 DN:1 A:3 T1q ON:3< B:4 QK:1> A:4 T2 PV:0 PV:1 A:5 T1k B:5 AT:0< PV:2
        A:0 B:0 B:1 A:1 AT:1< A:2 B:2 T1k A:3 B:3 T1q QK:2> PV:3 A:4 T2 B:4 B:5 A:5
        B:0 A:0 V:2> T1q B:1 QK:3> T2 B:2 A:1 B:3 T1k B:4 A:2 V:3> A:3 OP:0< A:4 PV:4 B:5 A:5 OP:1<
        B:0 ON:0 B:1 PV:5 PV:6 B:2 A:0 B:3 T1q T1k A:1 A:2 A:3 T2 PV:7 B:4 A:4 A:5 B:5
        ON:1 B:0 A:0 B:1 T1q B:2 A:1 B:3 A:2 PV:8 T2 A:3 A:4 B:4 T1k B:5 A:5 PV:9
        A:0 B:0 B:1 G:0> A:1 A:2 PV:10 U:0> B:2 B:3 T1k A:3 G:1> B:4 PV:11 U:1> T2 T1q A:4 A:5 B:5
    """,
    "act": """
        G:2 HL:1 HIq B:0 B:1 B:2 T1q G:3 B:3 HL:2 T1k G:4 B:4 T2 B:5 HL:3
        B:0 HIq G:5 HL:4 T1q B:1 B:2 PV:15< HL:5 B:3 T1k B:4 XT:0> XT:1> T2 B:5
        HIq DN:0 B:0 B:1 B:2 B:3 DN:1 T1q B:4 T2 T1k B:5
        AT:0< B:0 B:1 AT:1< HIq B:2 T1k T1q B:3 T2 PV:3 B:4 B:5
        B:0 HIq T1q B:1 B:2 T2 B:3 B:4 T1k B:5
        B:0 B:1 HIq B:2 B:3 T1q T1k T2 PV:7 B:4 B:5
        HIq B:0 B:1 T1q B:2 B:3 T2 B:4 T1k B:5
        B:0 G:0> B:1 B:2 T1k HIq B:3 G:1> B:4 T2 T1q HL:0> PV:11 B:5
    """,
    "dve": """
        G:2 A:0 ON:2< HL:1 A:1 LOq U:2 ST:0> G:3 A:2 A:3 U:3 HL:2 A:4 A:5 G:4 U:4 HL:3 LOk MX
        A:0 G:5 A:1 U:5 A:2 HL:4 HL:5 A:3 XT:0> A:4 XT:1> LOq A:5 V:0> MX LOk
        DN:0 A:0 QK:0> A:1 A:2 V:1> LOk DN:1 A:3 LOq A:4 QK:1> ON:3< A:5 MX
        A:0 AT:0< A:1 AT:1< A:2 QK:2> A:3 A:4 A:5 LOq V:2> LOk MX
        A:0 QK:3> LOq A:1 V:3> A:2 A:3 OP:0< A:4 A:5 OP:1< AD:0< MX LOk
        ON:0 AD:1< A:0 LOq A:1 A:2 A:3 A:4 LOk A:5 ON:1 MX
        A:0 A:1 A:2 A:3 LOk A:4 LOq A:5 MX
        A:0 G:0> A:1 U:0> A:2 A:3 G:1> LOq A:4 U:1> A:5 HL:0> MX LOk
    """,
    "pool": """
        HIk B:0 B:1 B:2 RS:0> B:3 NM:0> NM:1> NM:2> B:4 B:5
        HIk B:0 NM:3> B:1 B:2 B:3 B:4 B:5
        HIk B:0 ROPE:0> ROPE:1> B:1 B:2 B:3 ROPE:2> B:4 ROPE:3> ROPE:4> B:5 ROPE:5> ROPE:6>
        HIk ROPE:7> B:0 B:1 B:2 ROPE:8> B:3 ROPE:9> B:4 B:5 ROPE:10>
        B:0 B:1 ROPE:11> HIk ROPE:12> ROPE:13> B:2 B:3 B:4 ROPE:14> ROPE:15> B:5
        B:0 AD:0< HIk B:1 B:2 B:3 AD:1< B:4 B:5
        HIk B:0 B:1 B:2 B:3 B:4 B:5
        B:0 B:1 B:2 B:3 HIk B:4 B:5
    """,
}


def steps(engine, b):
    items = []
    for s, line in enumerate(SCHEDULE[engine].strip().splitlines()):
        for token in line.split():
            kind, _, index = token.rstrip("<>").partition(":")
            index = int(index or 0)
            if kind in AHEAD:
                n = b * PAIRS + s + AHEAD[kind]
                items.append((kind, n // PAIRS, n % PAIRS * (CHUNKS if kind in ("A", "B") else 1) + index))
            else:
                items.append((kind, b + token.count(">") - token.count("<"), index))
    return items


def plan(engine, b):
    if b < 0:
        return [(kind, 0, int(index or 0)) for kind, _, index in (t.partition(":") for t in START[engine].split())]
    return [item for item in steps(engine, b) if 0 <= item[1] < BATCH]


class Bank:

    def __init__(self):
        self.of, full, kinds, seen = {}, {"act": 0, "dve": 0}, {}, {}
        for b in range(-1, BATCH + 1):
            segment = plan("pe", b)
            places = [i for i in (steps("pe", b) if b >= 0 else segment) if i[0] in WORK]
            for item in segment:
                if item[0] in WORK:
                    kind, first = item[0], WORK[item[0]][0]
                    at = places.index(item) % WORK_BANKS
                    full[first] += 1
                    kinds[kind] = kinds.get(kind, 0) + 1
                    self.of[item] = (at, full[first], seen.get(at))
                    seen[at] = (kind, kinds[kind])
        middle = [i[0] for i in plan("pe", 2) if i[0] in WORK]
        self.full_per = {e: sum(WORK[k][0] == e for k in middle) for e in full}
        self.kind_per = {k: middle.count(k) for k in WORK}
        for one, two in zip(plan("pe", 1) + plan("pe", 2), plan("pe", 3) + plan("pe", 4)):
            if one[0] in WORK:
                a, b = self.of[one], self.of[two]
                assert a[0] == b[0] and b[1] - a[1] == 2 * self.full_per[WORK[one[0]][0]]
                assert a[2][0] == b[2][0] and b[2][1] - a[2][1] == 2 * self.kind_per[a[2][0]]


def build(nc, x, wq, bq, wk, bk, wv, bv, wo, bo, w_gate, w_up, w_down, consts, out):
    with ExitStack() as ctx:
        def sb(name, shape, dt):
            return ctx.enter_context(nc.sbuf_tensor(name, shape, dt))

        def sem(name):
            return ctx.enter_context(nc.semaphore(name))

        cst = sb("cst", [P, C_ALL], F32)
        ident = cst[:, C_ID:C_ID + P]
        ident_r = sb("ident_r", [P, P], F32R)
        bias3 = sb("bias3", [P, 3 * DM], F32)
        bo_row = sb("bo_row", [P, DM], F32)
        w3_hi = sb("w3_hi", [P, KT, 3 * DM], F32R)
        w3_lo = sb("w3_lo", [P, KT, 3 * DM], F32R)
        wo_hi = sb("wo_hi", [P, KT, DM], F32R)
        wo_lo = sb("wo_lo", [P, KT, DM], F32R)
        wgu_hi = sb("wgu_hi", [P, 2, KT, HID], F32R)
        wgu_lo = sb("wgu_lo", [P, 2, KT, HID], F32R)
        wd_hi = sb("wd_hi", [P, HT, DM], F32R)
        wd_lo = sb("wd_lo", [P, HT, DM], F32R)
        xn = sb("xn", [P, TT, DM], F32)
        stats = sb("stats", [P, TT, 6], F32)
        mean_var = sb("mean_var", [P, TT, 2], F32)
        rstd = sb("rstd", [P, TT], F32)
        minus_half = sb("minus_half", [P, TT], F32)
        xt_hi = sb("xt_hi", [P, KT, SEQ], F32R)
        xt_lo = sb("xt_lo", [P, KT, SEQ], F32R)
        qk_raw = sb("qk_raw", [P, 2, 2 * DM], F32)
        rope_b = sb("rope_b", [P, 2 * DM], F32)
        rot = sb("rot", [P, 2, TT, 2 * DM], F32)
        vals = sb("vals", [P, 2, TT, 288], F32)
        q_nat = sb("q_nat", [P, 4, TT, 2, ST], F32R)
        k_nat = sb("k_nat", [P, 2, TT, 2, ST], F32R)
        q_st = sb("q_st", [P, 2, SEQ], F32R)
        q_st2 = sb("q_st2", [P, 2, SEQ], F32R)
        k_st = sb("k_st", [P, 4, SEQ], F32R)
        row_max = sb("row_max", [P, 2, TT, 2], F32)
        probs = sb("probs", [P, 2 * SLOTS, SEQ], F32)
        o_t = sb("o_t", [P, SEQ], F32)
        inv_sum = sb("inv_sum", [P, TT, 4], F32)
        attn = sb("attn", [P, TT, DM], F32)
        at_hi = sb("at_hi", [P, KT, SEQ], F32R)
        at_lo = sb("at_lo", [P, KT, SEQ], F32R)
        hid = sb("hid", [P, 2, SEQ], F32)
        h_hi = sb("h_hi", [P, HT, SEQ], F32R)
        h_lo = sb("h_lo", [P, HT, SEQ], F32R)
        gate = sb("gate", [P, 2, TT // 2, 2 * DM], F32)
        res = sb("res", [P, TT, DM], F32)
        square = sb("square", [P, 4], F32)
        flag_i = sb("flag_i", [P, 1], I32)
        w3_raw = rot[:, 0, :, :].rearrange("p t c -> p (t c)")[:, 0:KT * 3 * DM].rearrange("p (k c) -> p k c", k=KT)
        wo_raw = rot[:, 1, :, :].rearrange("p t c -> p (t c)")[:, 0:KT * DM].rearrange("p (k c) -> p k c", k=KT)
        w_nat = probs[:, 0:9, :].rearrange("p (w a) c -> p w (a c)", w=3)

        ps_o = ctx.enter_context(nc.psum_tensor("ps_o", [P, SEQ], F32))
        ps_w = [ctx.enter_context(nc.psum_tensor(f"ps_w{i}", [P, SEQ], F32)) for i in range(WORK_BANKS)]

        const_in = sem("const_in"); bias_in = sem("bias_in"); w3_in = sem("w3_in"); wo_in = sem("wo_in"); ffn_w_in = sem("ffn_w_in"); x_in = sem("x_in")
        res_in = sem("res_in"); out_stored = sem("out_stored")
        full = {"act": sem("work_full_for_act"), "dve": sem("work_full_for_dve")}
        w3_hi_ready = sem("w3_hi_ready"); w3_ready = sem("w3_ready"); wo_ready = sem("wo_ready"); ffn_w_float = sem("ffn_w_float")
        wt_hi = sem("wt_hi"); wt_ready = sem("wt_ready"); squares_max = sem("squares_max"); all_max = sem("all_max"); flag_set = sem("flag_set")
        dve_passed = sem("dve_passed"); pool_passed = sem("pool_passed")
        set_once = sem("set_once"); half_set = sem("half_set")
        stats_ready = sem("stats_ready"); aggr_ready = sem("aggr_ready"); rstd_ready = sem("rstd_ready")
        xn_ready = sem("xn_ready")
        xt_hi_ready = sem("xt_hi_ready"); xt_ready = sem("xt_ready")
        qk_ready = sem("qk_ready"); v_ready = sem("v_ready"); rope_parts = sem("rope_parts"); start_parts = sem("start_parts"); rot_ready = sem("rot_ready")
        hi_q_ready = sem("hi_q_ready"); hi_k_ready = sem("hi_k_ready"); lo_q_ready = sem("lo_q_ready"); lo_k_ready = sem("lo_k_ready")
        q_st_ready = sem("q_st_ready"); k_st_ready = sem("k_st_ready"); q_st2_ready = sem("q_st2_ready")
        a_taken = sem("a_taken"); max_hi = sem("max_hi"); max_ready = sem("max_ready")
        exp_done = sem("exp_done"); masked_done = sem("masked_done")
        pv_done = sem("pv_done"); o_t_ready = sem("o_t_ready"); inv_ready = sem("inv_ready"); attn_ready = sem("attn_ready")
        at_hi_ready = sem("at_hi_ready"); at_ready = sem("at_ready"); sum_ready = sem("sum_ready"); prod_ready = sem("prod_ready"); res_ready = sem("res_ready")
        tanh_ready = sem("tanh_ready"); gated = sem("gated"); hid_ready = sem("hid_ready")
        h_hi_ready = sem("h_hi_ready"); h_ready = sem("h_ready"); silu_ready = sem("silu_ready")
        released = {"A": a_taken, "B": exp_done, "T2": q_st2_ready, "T1q": q_st_ready, "T1k": k_st_ready,
                    "XT": xt_ready, "QK": qk_ready, "V": v_ready,
                    "ON": attn_ready, "AT": at_ready, "OP": sum_ready, "G": gated, "U": hid_ready,
                    "DN": silu_ready, "WT": wt_ready}

        bank = Bank()
        MIDDLE = (BATCH - 2) // 2

        def need(eng, s, value, per_batch, it, apart=None):
            if it is not None:
                assert value > 0
                wait = eng.wait_ge(s, it * (2 * per_batch) + value)
                if apart:
                    wait.then_inc(apart, 1)
            elif value > 0:
                eng.wait_ge(s, value)

        def run(name, eng, do):
            for item in plan(name, -1) + plan(name, 0):
                do(item, None)
            with eng.Fori(0, MIDDLE) as it:
                for item in plan(name, 1) + plan(name, 2):
                    do(item, it)
            for item in plan(name, BATCH - 1) + plan(name, BATCH):
                do(item, None)

        def wait_full(eng, name, item, it, apart=None):
            need(eng, full[name], bank.of[item][1], bank.full_per[name], it, apart)

        def w_of(item):
            return ps_w[bank.of[item][0]]

        def wt_cols(i):
            return P * (2 if i < 8 and i % 2 else 4)

        def wt_view(gate_up, down, i):
            if i < 8:
                w, k, half = i // 4, i // 2 % 2, i % 2
                return gate_up[:, w, k, half * 512:half * 512 + wt_cols(i)]
            return down[:, 2 * (i - 8):2 * (i - 8) + 2, :].rearrange("p j d -> p (j d)")

        def tanh_at(b, j):
            return b * (HT + 2) + j + 1

        def rot_of(b, pair, which):
            c = which * DM + pair * 2 * HD
            return rot[:, b % 2, :, c:c + 2 * HD].rearrange("p t (h c) -> p t h c", h=2)

        def add_x(eng, tensor_tensor, item, it):
            kind, b, i = item
            need(eng, prod_ready, 2 * b + i + 1, 2, it)
            if i == 0:
                need(eng, res_in, 16 * (b + 1), 16, it)
            r = res[:, 2 * i:2 * i + 2, :].rearrange("p t d -> p (t d)")
            tensor_tensor(r, r, hid[:, i, :], ALU.add).then_inc(res_ready, 1)

        def normalise(eng, tensor_scalar, passed, item, it):
            kind, b, i = item
            if i == 0:
                need(eng, rstd_ready, 2 * b + 2, 2, it, apart=passed)
            tensor_scalar(xn[:, i, :], xn[:, i, :], mean_var[:, i, 0:1], rstd[:, i:i + 1],
                          ALU.subtract, ALU.mult).then_inc(xn_ready, 1)

        def rotate(eng, tensor_tensor, item, it):
            kind, b, i = item
            t, part = divmod(i, 4)
            src, dst = qk_raw[:, t % 2, :], rot[:, b % 2, t, :]
            if b == 0 and t >= DVE_ROTATES:
                swapped, parts, parts_done = attn[:, 0:2, :].rearrange("p t d -> p (t d)"), start_parts, 3 * (t + 1 - DVE_ROTATES)
            else:
                swapped, parts, parts_done = rope_b[:], rope_parts, 3 * (b * TT + t + 1) - (3 * (TT - DVE_ROTATES) if b else 0)
            by_head = lambda ap: ap.rearrange("p (h c) -> p h c", c=HD)
            by_two = lambda ap: ap.rearrange("p (h j e) -> p h j e", j=HD // 2, e=2)
            cos = cst[:, C_COS + t * HD:C_COS + (t + 1) * HD].rearrange("p (a c) -> p a c", a=1).broadcast_to([P, 2 * HEADS, HD])
            sin = cst[:, C_SIN + t * HD:C_SIN + (t + 1) * HD].rearrange("p (a j e) -> p a j e", a=1, e=2)\
                .broadcast_to([P, 2 * HEADS, HD // 2, 2])
            if part == 0:
                need(eng, qk_ready, b * TT + t + 1, TT, it)
                tensor_tensor(by_head(dst), by_head(src), cos, ALU.mult).then_inc(parts, 1)
            elif part < 3:
                e = part - 1
                if e == 0:
                    need(eng, rot_ready, b * TT + t, TT, it)
                tensor_tensor(by_two(swapped)[:, :, :, e], by_two(src)[:, :, :, 1 - e], sin[:, :, :, e],
                              ALU.mult).then_inc(parts, 1)
            else:
                need(eng, parts, parts_done, 3 * TT, it)
                tensor_tensor(dst, dst, swapped, ALU.add).then_inc(rot_ready, 1)

        def high_parts(name, eng, copy, passed, item, it):
            kind, b, i = item
            if HI_ENGINE[kind] != name:
                return
            n = b * PAIRS + i
            if i == 0:
                need(eng, rot_ready, (b + 1) * TT, TT, it)
            if kind == "HIq":
                need(eng, q_st2_ready, n - 3, PAIRS, it, apart=passed)
            else:
                need(eng, k_st_ready, n - 1, PAIRS, it, apart=passed)
            nat, which, places, ready = (q_nat[:, i % 4], 0, (0, 1), hi_q_ready) if kind == "HIq" else (k_nat[:, i % 2], 1, (0, 2), hi_k_ready)
            for at in places:
                copy(nat[:, :, :, at * HD:(at + 1) * HD], rot_of(b, i, which)).then_inc(ready, 1)

        BIAS_LOADS = 4
        block = ctx.enter_context(nc.Block())

        @block.sync
        def _(sp):
            by_tile = lambda ap: ap.rearrange("(t p) d -> p t d", p=P)
            sp.dma_start(xn[:], by_tile(x[0])).then_inc(x_in, 16)
            sp.dma_start(cst[:], consts).then_inc(const_in, 16)
            for dst, v in [(bias3[:, j * DM:(j + 1) * DM], v) for j, v in enumerate((bq, bk, bv))] + [(bo_row[:], bo)]:
                sp.dma_start(dst,
                             v.rearrange("(a d) -> a d", a=1).broadcast_to([P, DM])).then_inc(bias_in, 16)
            for j, w in enumerate((w_gate, w_up)):
                sp.dma_start(w_nat[:, j, :].bitcast(I32).rearrange("p (t d) -> p t d", d=DM), by_tile(w)).then_inc(ffn_w_in, 16)
            sp.dma_start(w_nat[:, 2, :].bitcast(I32).rearrange("p (t d) -> p t d", d=HID), by_tile(w_down)).then_inc(ffn_w_in, 16)
            sp.dma_start(res[:], by_tile(x[0])).then_inc(res_in, 16)
            sp.wait_ge(xt_ready, KT)
            sp.dma_start(xn[:], by_tile(x[1])).then_inc(x_in, 16)
            with sp.Fori(1, BATCH - 1) as b:
                sp.wait_ge(xt_ready, b * KT + KT)
                sp.dma_start(xn[:], x[bass.ds(b + 1, 1), :, :].rearrange("a (t p) d -> p (a t) d", p=P)).then_inc(x_in, 16)
                sp.wait_ge(res_ready, b * 2)
                sp.dma_start(out[bass.ds(b - 1, 1), :, :].rearrange("a (t p) d -> p (a t) d", p=P), res[:]).then_inc(out_stored, 16)
                sp.wait_ge(out_stored, b * 16)
                sp.dma_start(res[:], x[bass.ds(b, 1), :, :].rearrange("a (t p) d -> p (a t) d", p=P)).then_inc(res_in, 16)
            for b in (BATCH - 2, BATCH - 1):
                sp.wait_ge(res_ready, (b + 1) * 2)
                sp.dma_start(by_tile(out[b]), res[:]).then_inc(out_stored, 16)
                sp.wait_ge(out_stored, (b + 1) * 16)
                if b + 1 < BATCH:
                    sp.dma_start(res[:], by_tile(x[b + 1])).then_inc(res_in, 16)

        @block.tensor
        def _(pe):
            flag = {}

            def take_bank(item, it):
                before = bank.of[item][2]
                if before:
                    need(pe, released[before[0]], before[1], bank.kind_per[before[0]], it)
                return w_of(item)

            def done(ins, item):
                ins.then_inc(full[WORK[item[0]][0]], 1)

            def group(dst, terms, middle=()):
                for i, (w, m) in enumerate(terms):
                    if middle and i == 1:
                        with pe.If(flag["has_lo"] > 0):
                            for wl, ml in middle:
                                pe.matmul(dst, wl, ml, start=False, stop=False)
                    last = pe.matmul(dst, w, m, start=(i == 0), stop=(i == len(terms) - 1))
                return last

            def do(item, it):
                kind, b, i = item
                n = b * PAIRS + i
                if kind == "WQ":
                    pe.wait_ge(const_in, 16)
                elif kind == "WC":
                    pe.wait_ge(set_once, 5)
                elif kind == "XT":
                    need(pe, xn_ready, (b + 1) * TT, TT, it)
                    dst = take_bank(item, it)
                    for tt in range(TT):
                        last = pe.transpose(dst[:, tt * P:(tt + 1) * P], xn[:, tt, i * P:(i + 1) * P], ident)
                    done(last, item)
                elif kind in ("QK", "V"):
                    if i == 0:
                        need(pe, xt_ready, (b + 1) * KT, KT, it)
                        if b == 0:
                            pe.wait_ge(w3_ready, 1)
                    dst = take_bank(item, it)
                    c0, c1 = (0, 2 * DM) if kind == "QK" else (2 * DM, 3 * DM)
                    tok = slice(i * P, (i + 1) * P)
                    terms = []
                    for k in range(KT):
                        terms += [(xt_hi[:, k, tok], w3_hi[:, k, c0:c1]), (xt_hi[:, k, tok], w3_lo[:, k, c0:c1]),
                                  (xt_lo[:, k, tok], w3_hi[:, k, c0:c1])]
                    done(group(dst[:, 0:c1 - c0], terms), item)
                elif kind == "WT":
                    if i == 0:
                        pe.wait_ge(ffn_w_float, 3)
                    dst = take_bank(item, it)
                    if i < 8:
                        w, k, half = i // 4, i // 2 % 2, i % 2
                        for a, t in enumerate(range(4 * half, min(4 * half + 4, HT))):
                            last = pe.transpose(dst[:, a * P:(a + 1) * P], w_nat[:, w, t * DM + k * P:t * DM + (k + 1) * P], ident)
                    else:
                        for a, (j, m) in enumerate([(2 * (i - 8) + jj, m) for jj in range(2) for m in range(KT)]):
                            last = pe.transpose(dst[:, a * P:(a + 1) * P], w_nat[:, 2, m * HID + j * P:m * HID + (j + 1) * P], ident)
                    done(last, item)
                elif kind == "FLAG":
                    pe.wait_ge(flag_set, 1)
                    flag["has_lo"] = pe.value_load(flag_i[0:1, 0:1], min_val=0, max_val=1)
                elif kind in ("T1q", "T1k"):
                    need(pe, lo_q_ready if kind == "T1q" else lo_k_ready, n + 1, PAIRS, it)
                    dst = take_bank(item, it)
                    for tt in range(TT):
                        src = (q_nat[:, i % 4, tt] if kind == "T1q" else k_nat[:, i % 2, tt]).rearrange("p h c -> p (h c)")
                        last = pe.transpose(dst[:, tt * P:(tt + 1) * P].bitcast(F32R), src, ident_r[:])
                    done(last, item)
                elif kind == "T2":
                    need(pe, max_ready, n + 1, PAIRS, it)
                    dst = take_bank(item, it)
                    for tt in range(TT):
                        last = pe.transpose(dst[:, tt * P:(tt + 1) * P].bitcast(F32R), q_nat[:, i % 4, tt].rearrange("p h c -> p (h c)"), ident_r[:])
                    done(last, item)
                elif kind == "A":
                    pair, c = divmod(i, CHUNKS)
                    m = b * PAIRS * CHUNKS + i
                    if c == 0:
                        need(pe, q_st_ready, b * PAIRS + pair + 1, PAIRS, it)
                        need(pe, k_st_ready, b * PAIRS + pair + 1, PAIRS, it)
                    dst = take_bank(item, it)
                    for h, qt, col in A_PARTS[c]:
                        rows = slice(h * ST, h * ST + 3 * HD)
                        w = (qt + 1) * P
                        last = pe.matmul(dst[:, col:col + w], q_st[rows, pair % 2, qt * P:(qt + 1) * P],
                                         k_st[rows, pair % 4, 0:w], start=True, stop=True)
                    done(last, item)
                elif kind == "B":
                    pair, c = divmod(i, CHUNKS)
                    if c == 0:
                        need(pe, q_st2_ready, b * PAIRS + pair + 1, PAIRS, it)
                    dst = take_bank(item, it)
                    for h, kt, col in B_PARTS[c]:
                        rows = slice(h * ST, (h + 1) * ST)
                        w = SEQ - kt * P
                        last = pe.matmul(dst[:, col:col + w], k_st[rows, pair % 4, kt * P:(kt + 1) * P],
                                         q_st2[rows, pair % 2, kt * P:SEQ], start=True, stop=True)
                    done(last, item)
                elif kind == "PV":
                    group_, step = divmod(i, TT)
                    g, kt = b * GROUPS + group_, PV_ORDER[step]
                    if step == 0:
                        need(pe, o_t_ready, g, GROUPS, it)
                        if group_ == 0:
                            need(pe, v_ready, (b + 1) * TT, TT, it)
                    if step != 2:
                        need(pe, masked_done, CHUNKS * (2 * g + 1) + (2, 4, 0, 6)[step], PAIRS * CHUNKS, it)
                    for hh in range(4):
                        slot, col = P_AT[kt][hh % 2]
                        head = 4 * group_ + hh
                        last = pe.matmul(ps_o[32 * hh:32 * hh + 32, kt * P:SEQ],
                                         vals[:, b % 2, kt, head * VW:head * VW + 32],
                                         probs[:, (hh // 2) * SLOTS + slot, col:col + SEQ - kt * P],
                                         start=(step == 0), stop=(step == TT - 1), skip_group_check=True)
                    last.then_inc(pv_done, 1)
                elif kind == "ON":
                    need(pe, o_t_ready, b * GROUPS + i + 1, GROUPS, it)
                    dst = take_bank(item, it)
                    for tt in range(TT):
                        last = pe.transpose(dst[:, tt * P:(tt + 1) * P], o_t[:, tt * P:(tt + 1) * P], ident)
                    done(last, item)
                elif kind == "AT":
                    need(pe, attn_ready, b * GROUPS + (GROUPS // KT) * (i + 1), GROUPS, it)
                    dst = take_bank(item, it)
                    for tt in range(TT):
                        last = pe.transpose(dst[:, tt * P:(tt + 1) * P], attn[:, tt, i * P:(i + 1) * P], ident)
                    done(last, item)
                elif kind == "OP":
                    if b == 0 and i == 0:
                        pe.wait_ge(wo_ready, 1)
                    need(pe, at_ready, (b + 1) * KT, KT, it)
                    dst = take_bank(item, it)
                    for a in range(2):
                        tok = slice((2 * i + a) * P, (2 * i + a + 1) * P)
                        terms = []
                        for k in range(KT):
                            terms += [(at_hi[:, k, tok], wo_hi[:, k, :]), (at_hi[:, k, tok], wo_lo[:, k, :]),
                                      (at_lo[:, k, tok], wo_hi[:, k, :])]
                        last = group(dst[:, a * DM:(a + 1) * DM], terms)
                    done(last, item)
                elif kind in ("G", "U"):
                    if kind == "G" and i == 0:
                        need(pe, xt_ready, (b + 1) * KT, KT, it)
                    dst = take_bank(item, it)
                    w, col = (0 if kind == "G" else 1), slice(i * P, (i + 1) * P)
                    terms = [(wgu_hi[:, w, k, col], xt[:, k, :]) for k in range(KT) for xt in (xt_hi, xt_lo)]
                    low = [(wgu_lo[:, w, k, col], xt_hi[:, k, :]) for k in range(KT)]
                    done(group(dst[:, :], terms, low), item)
                elif kind == "DN":
                    need(pe, h_ready, (b + 1) * HT, HT, it)
                    dst = take_bank(item, it)
                    for a in range(2):
                        tok = slice((2 * i + a) * P, (2 * i + a + 1) * P)
                        terms = [(h[:, j, tok], wd_hi[:, j, :]) for j in range(HT) for h in (h_hi, h_lo)]
                        low = [(h_hi[:, j, tok], wd_lo[:, j, :]) for j in range(HT)]
                        last = group(dst[:, a * DM:(a + 1) * DM], terms, low)
                    done(last, item)

            run("pe", pe, do)

        @block.scalar
        def _(act):
            def do(item, it):
                kind, b, i = item
                n = b * PAIRS + i
                if kind == "WQ":
                    for j, w in enumerate((wq, wk, wv)):
                        act.dma_start(w3_raw[:, :, j * DM:(j + 1) * DM], w.rearrange("(t p) d -> p t d", p=P)).then_inc(w3_in, 16)
                    act.dma_start(wo_raw, wo.rearrange("(t p) d -> p t d", p=P)).then_inc(wo_in, 16)
                    act.wait_ge(w3_in, 48)
                    nc.scalar.copy(w3_hi[:], w3_raw).then_inc(w3_hi_ready, 1)
                    act.wait_ge(wo_in, 16)
                    nc.scalar.copy(wo_hi[:], wo_raw).then_inc(w3_hi_ready, 1)
                elif kind == "WC":
                    act.wait_ge(ffn_w_in, 48)
                    for w in range(3):
                        nc.scalar.copy(w_nat[:, w, :], w_nat[:, w, :].bitcast(I32)).then_inc(ffn_w_float, 1)
                elif kind == "XT":
                    wait_full(act, "act", item, it)
                    nc.scalar.copy(xt_hi[:, i, :], w_of(item)[:, :]).then_inc(xt_hi_ready, 1)
                elif kind == "WT":
                    wait_full(act, "act", item, it)
                    nc.scalar.copy(wt_view(wgu_hi, wd_hi, i), w_of(item)[:, 0:wt_cols(i)]).then_inc(wt_hi, 1)
                elif kind in ("T1q", "T1k", "T2"):
                    wait_full(act, "act", item, it)
                    dst, ready = {"T1q": (q_st[:, i % 2, :], q_st_ready), "T1k": (k_st[:, i % 4, :], k_st_ready),
                                  "T2": (q_st2[:, i % 2, :], q_st2_ready)}[kind]
                    nc.scalar.copy(dst, w_of(item)[:, :]).then_inc(ready, 1)
                elif kind in ("HIq", "HIk"):
                    high_parts("act", act, nc.scalar.copy, None, item, it)
                elif kind == "B":
                    pair, c = divmod(i, CHUNKS)
                    m = b * PAIRS * CHUNKS + i
                    wait_full(act, "act", item, it)
                    if pair % 2 == 0 and c % 2 == 0:
                        need(act, pv_done, TT * ((b * PAIRS + pair) // 2 - 1) + (1, 3, 4)[c // 2], TT * GROUPS, it)
                    slot, col = slot_of(c)
                    nc.scalar.activation(probs[:, (pair % 2) * SLOTS + slot, col:col + WIDTH[c]], w_of(item)[:, 0:WIDTH[c]], ACT.Exp,
                                         scale=QSCALE).then_inc(exp_done, 1)
                elif kind == "PV" and i % TT == TT - 1:
                    need(act, pv_done, b * GROUPS * TT + i + 1, GROUPS * TT, it)
                    nc.scalar.copy(o_t[:, :], ps_o[:, :]).then_inc(o_t_ready, 1)
                elif kind == "AT":
                    wait_full(act, "act", item, it)
                    nc.scalar.copy(at_hi[:, i, :], w_of(item)[:, :]).then_inc(at_hi_ready, 1)
                elif kind == "G":
                    wait_full(act, "act", item, it)
                    if i >= 2:
                        need(act, h_ready, b * HT + i - 1, HT, it)
                    elif b:
                        need(act, silu_ready, b * 2, 2, it)
                        if b > 1:
                            need(act, res_ready, 2 * (b - 1), 2, it)
                    nc.scalar.activation(hid[:, i % 2, :], w_of(item)[:, :], ACT.Tanh,
                                         scale=0.5 * WSCALE).then_inc(tanh_ready, 1)
                elif kind == "HL":
                    need(act, hid_ready, b * HT + i + 1, HT, it)
                    nc.scalar.copy(h_hi[:, i, :], hid[:, i % 2, :]).then_inc(h_hi_ready, 1)
                elif kind == "DN":
                    wait_full(act, "act", item, it)
                    nc.scalar.activation(hid[:, i, :], w_of(item)[:, :], ACT.Tanh,
                                         scale=0.5 * WSCALE).then_inc(tanh_ready, 1)

            run("act", act, do)

        @block.vector
        def _(dve):
            def do(item, it):
                kind, b, i = item
                n = b * PAIRS + i
                if kind == "WQ":
                    nc.vector.memset(q_nat[:, :, :, :, 3 * HD:ST].bitcast(F32), 0.0).then_inc(set_once, 1)
                    nc.vector.memset(k_nat[:, :, :, :, 3 * HD:ST].bitcast(F32), 1.0).then_inc(set_once, 1)
                    nc.vector.memset(vals[:, :, :, 0:HEADS * VW].rearrange("p b t (h c) -> p (b t) h c", c=VW)[:, :, :, HD], 1.0)\
                        .then_inc(set_once, 1)
                    nc.vector.memset(vals[:, :, :, HEADS * VW:], 1.0).then_inc(set_once, 1)
                    dve.wait_ge(const_in, 16)
                    nc.vector.tensor_copy(ident_r[:], ident).then_inc(set_once, 1)
                elif kind == "WC":
                    dve.wait_ge(w3_hi_ready, 1)
                    nc.vector.tensor_tensor(w3_lo[:], w3_raw, w3_hi[:].bitcast(F32), ALU.subtract).then_inc(w3_ready, 1)
                    dve.wait_ge(bias_in, 16 * BIAS_LOADS)
                elif kind == "SQ":
                    dve.wait_ge(ffn_w_float, 3)
                    for w in range(3):
                        if w:
                            dve.wait_ge(squares_max, w)
                        nc.vector.tensor_tensor_reduce(out=h_lo[:, 0:3, :].rearrange("p j c -> p (j c)"),
                                                       in0=w_nat[:, w, :], in1=w_nat[:, w, :], scale=1.0, scalar=0.0,
                                                       op0=ALU.mult, op1=ALU.max, accum_out=square[:, w:w + 1])\
                            .then_inc(squares_max, 1)
                    dve.wait_ge(squares_max, 3)
                    nc.vector.tensor_reduce(square[:, 3:4], square[:, 0:3], AX.X, ALU.max).then_inc(squares_max, 1)
                elif kind == "FLAG":
                    dve.wait_ge(all_max, 1)
                    nc.vector.tensor_scalar(flag_i[:], square[:, 0:1], float(1 << 24), None, ALU.is_gt).then_inc(flag_set, 1)
                elif kind == "ST":
                    need(dve, x_in, 16 * (b + 1), 16, it)
                    need(dve, aggr_ready, TT * b, TT, it)
                    for tt in range(TT):
                        nc.vector.bn_stats(stats[:, tt, :], xn[:, tt, :]).then_inc(stats_ready, 1)
                    need(dve, stats_ready, TT * (b + 1), TT, it, apart=dve_passed)
                    for tt in range(TT):
                        nc.vector.bn_aggr(mean_var[:, tt, :], stats[:, tt, :]).then_inc(aggr_ready, 1)
                elif kind == "NM" and b == 0:
                    normalise(dve, nc.vector.tensor_scalar, dve_passed, item, it)
                elif kind == "XT":
                    need(dve, xt_hi_ready, b * KT + i + 1, KT, it)
                    nc.vector.tensor_tensor(xt_lo[:, i, :], w_of(item)[:, :], xt_hi[:, i, :].bitcast(F32), ALU.subtract)\
                        .then_inc(xt_ready, 1)
                elif kind == "QK":
                    wait_full(dve, "dve", item, it)
                    need(dve, rot_ready, b * TT + i - 1, TT, it)
                    nc.vector.tensor_tensor(qk_raw[:, i % 2, :], w_of(item)[:, :], bias3[:, 0:2 * DM], ALU.add)\
                        .then_inc(qk_ready, 1)
                elif kind == "V":
                    wait_full(dve, "dve", item, it)
                    v3 = vals[:, b % 2, i, 0:HEADS * VW].rearrange("p (h c) -> p h c", c=VW)[:, :, 0:HD]
                    nc.vector.tensor_tensor(v3, w_of(item)[:, 0:DM].rearrange("p (h c) -> p h c", c=HD),
                                            bias3[:, 2 * DM:3 * DM].rearrange("p (h c) -> p h c", c=HD), ALU.add)\
                        .then_inc(v_ready, 1)
                elif kind == "WT":
                    dve.wait_ge(wt_hi, i + 1)
                    hi, lo = wt_view(wgu_hi, wd_hi, i), wt_view(wgu_lo, wd_lo, i)
                    nc.vector.tensor_tensor(lo, w_of(item)[:, 0:wt_cols(i)], hi.bitcast(F32), ALU.subtract)\
                        .then_inc(wt_ready, 1)
                elif kind == "ROPE":
                    rotate(dve, nc.vector.tensor_tensor, item, it)
                elif kind in ("HIq", "HIk"):
                    high_parts("dve", dve, nc.vector.tensor_copy, dve_passed, item, it)
                elif kind == "LOq":
                    need(dve, hi_q_ready, 2 * (n + 1), 2 * PAIRS, it)
                    qn = q_nat[:, i % 4, :, :, :]
                    nc.vector.tensor_tensor(qn[:, :, :, 2 * HD:3 * HD], rot_of(b, i, 0), qn[:, :, :, 0:HD].bitcast(F32), ALU.subtract)\
                        .then_inc(lo_q_ready, 1)
                elif kind == "LOk":
                    need(dve, hi_k_ready, 2 * (n + 1), 2 * PAIRS, it)
                    kn = k_nat[:, i % 2, :, :, :]
                    nc.vector.tensor_tensor(kn[:, :, :, HD:2 * HD], rot_of(b, i, 1), kn[:, :, :, 0:HD].bitcast(F32), ALU.subtract)\
                        .then_inc(lo_k_ready, 1)
                elif kind == "A":
                    pair, c = divmod(i, CHUNKS)
                    m = b * PAIRS * CHUNKS + i
                    wait_full(dve, "dve", item, it, apart=dve_passed)
                    for h, qt, col in A_PARTS[c]:
                        w = (qt + 1) * P
                        last = nc.vector.tensor_tensor_reduce(
                            out=w_of(item)[:, col:col + w], in0=w_of(item)[:, col:col + w], in1=cst[:, C_MASK + SEQ - w:C_MASK + SEQ],
                            scale=1.0, scalar=-3e38, op0=ALU.add, op1=ALU.max, accum_out=row_max[:, pair % 2, qt, h:h + 1])
                    last.then_inc(a_taken, 1)
                elif kind == "MX":
                    need(dve, a_taken, (n + 1) * CHUNKS, PAIRS * CHUNKS, it)
                    mx, qn = row_max[:, i % 2, :, :], q_nat[:, i % 4, :, :, :]
                    nc.vector.tensor_scalar(qn[:, :, :, 3 * HD], mx, -1.0, None, ALU.mult).then_inc(max_hi, 1)
                    need(dve, max_hi, n + 1, PAIRS, it)
                    nc.vector.scalar_tensor_tensor(out=qn[:, :, :, 3 * HD + 1], in0=mx, scalar=-1.0, in1=qn[:, :, :, 3 * HD].bitcast(F32),
                                                   op0=ALU.mult, op1=ALU.subtract).then_inc(max_ready, 1)
                elif kind == "ON":
                    wait_full(dve, "dve", item, it)
                    o4 = w_of(item)[:, :].rearrange("p (t h c) -> p t h c", t=TT, h=4)
                    g = b * GROUPS + i
                    need(dve, attn_ready, g, GROUPS, it)
                    nc.vector.reciprocal(inv_sum[:], o4[:, :, :, HD]).then_inc(inv_ready, 1)
                    need(dve, inv_ready, g + 1, GROUPS, it)
                    nc.vector.tensor_tensor(attn[:, :, i * 64:(i + 1) * 64].rearrange("p t (h c) -> p t h c", h=4),
                                            o4[:, :, :, 0:HD], inv_sum[:].rearrange("p t (h a) -> p t h a", a=1)
                                            .broadcast_to([P, TT, 4, HD]), ALU.mult).then_inc(attn_ready, 1)
                elif kind == "AT":
                    need(dve, at_hi_ready, b * KT + i + 1, KT, it)
                    nc.vector.tensor_tensor(at_lo[:, i, :], w_of(item)[:, :], at_hi[:, i, :].bitcast(F32), ALU.subtract)\
                        .then_inc(at_ready, 1)
                elif kind == "OP":
                    wait_full(dve, "dve", item, it)
                    nc.vector.tensor_tensor(hid[:, i, :].rearrange("p (a d) -> p a d", a=2), w_of(item)[:, :].rearrange("p (a d) -> p a d", a=2),
                                            bo_row[:].rearrange("p (a d) -> p a d", a=1).broadcast_to([P, 2, DM]), ALU.add).then_inc(sum_ready, 1)
                    need(dve, sum_ready, 2 * b + i + 1, 2, it)
                    nc.vector.scalar_tensor_tensor(out=hid[:, i, :], in0=hid[:, i, :], scalar=0.5 * WSCALE, in1=gate[:, b % 2, i, :],
                                                   op0=ALU.mult, op1=ALU.mult).then_inc(prod_ready, 1)
                elif kind == "AD" and b == BATCH - 1:
                    add_x(dve, nc.vector.tensor_tensor, item, it)
                elif kind == "G":
                    need(dve, tanh_ready, tanh_at(b, i), HT + 2, it)
                    nc.vector.scalar_tensor_tensor(out=hid[:, i % 2, :], in0=hid[:, i % 2, :], scalar=1.0,
                                                   in1=w_of(item)[:, :], op0=ALU.add, op1=ALU.mult).then_inc(gated, 1)
                elif kind == "U":
                    wait_full(dve, "dve", item, it)
                    need(dve, gated, b * HT + i + 1, HT, it)
                    nc.vector.scalar_tensor_tensor(out=hid[:, i % 2, :], in0=w_of(item)[:, :], scalar=0.5 * WSCALE * WSCALE,
                                                   in1=hid[:, i % 2, :], op0=ALU.mult, op1=ALU.mult).then_inc(hid_ready, 1)
                elif kind == "HL":
                    need(dve, h_hi_ready, b * HT + i + 1, HT, it)
                    nc.vector.tensor_tensor(h_lo[:, i, :], hid[:, i % 2, :], h_hi[:, i, :].bitcast(F32), ALU.subtract)\
                        .then_inc(h_ready, 1)
                elif kind == "DN":
                    need(dve, tanh_ready, tanh_at(b, HT + i), HT + 2, it)
                    nc.vector.scalar_tensor_tensor(out=gate[:, b % 2, i, :], in0=hid[:, i, :], scalar=1.0,
                                                   in1=w_of(item)[:, :], op0=ALU.add, op1=ALU.mult).then_inc(silu_ready, 1)

            run("dve", dve, do)

        @block.gpsimd
        def _(pool):
            def do(item, it):
                kind, b, i = item
                n = b * PAIRS + i
                if kind == "WQ":
                    nc.gpsimd.memset(minus_half[:], -0.5).then_inc(half_set, 1)
                    pool.wait_ge(half_set, 1)
                elif kind == "RS":
                    need(pool, xn_ready, TT * b, TT, it)
                    need(pool, aggr_ready, TT * (b + 1), TT, it, apart=pool_passed)
                    nc.gpsimd.tensor_scalar(rstd[:], mean_var[:, :, 1], EPS, None, ALU.add).then_inc(rstd_ready, 1)
                    need(pool, rstd_ready, 2 * b + 1, 2, it)
                    nc.gpsimd.tensor_tensor(rstd[:], rstd[:], minus_half[:], ALU.pow).then_inc(rstd_ready, 1)
                elif kind == "AD" and b < BATCH - 1:
                    add_x(pool, nc.gpsimd.tensor_tensor, item, it)
                elif kind == "NM" and b > 0:
                    normalise(pool, nc.gpsimd.tensor_scalar, pool_passed, item, it)
                elif kind == "ROPE" and (b > 0 or i >= 4 * DVE_ROTATES):
                    rotate(pool, nc.gpsimd.tensor_tensor, item, it)
                elif kind in ("HIq", "HIk"):
                    high_parts("pool", pool, nc.gpsimd.tensor_copy, pool_passed, item, it)
                elif kind == "B":
                    pair, c = divmod(i, CHUNKS)
                    m = b * PAIRS * CHUNKS + i
                    need(pool, exp_done, m + 1, PAIRS * CHUNKS, it, apart=pool_passed)
                    blocks = [col for _, _, col in B_PARTS[c]]
                    slot, col = slot_of(c)
                    pr = probs[:, (pair % 2) * SLOTS + slot, col:col + WIDTH[c]]
                    if len(blocks) == 1:
                        v, pattern = pr[:, 0:P], [[1, P]]
                    else:
                        a = pr[:, 0:P]
                        ap = list(a.ap)
                        v = bass.AP(tensor=a.tensor, offset=a.offset, ap=[list(ap[0]), [blocks[1], 2], [1, P]])
                        pattern = [[0, 2], [1, P]]
                    nc.gpsimd.affine_select(out=v, in_=v, compare_op=ALU.is_ge, fill=0.0, base=0, pattern=pattern,
                                            channel_multiplier=-1).then_inc(masked_done, 1)
                elif kind == "WC":
                    pool.wait_ge(w3_hi_ready, 2)
                    nc.gpsimd.tensor_tensor(wo_lo[:], wo_raw, wo_hi[:].bitcast(F32), ALU.subtract).then_inc(wo_ready, 1)
                    pool.wait_ge(const_in, 16)
                    pool.wait_ge(set_once, 5)
                elif kind == "SQ":
                    pool.wait_ge(squares_max, 4)
                    nc.gpsimd.partition_all_reduce(square[:, 0:1], square[:, 3:4], P, bass.bass_isa.ReduceOp.max).then_inc(all_max, 1)

            run("pool", pool, do)


_INS = ["L0_attn_x", "L0_attn_wq", "L0_attn_bq", "L0_attn_wk", "L0_attn_bk", "L0_attn_wv", "L0_attn_bv", "L0_attn_wo",
        "L0_attn_bo", "L0_ffn_w_gate", "L0_ffn_w_up", "L0_ffn_w_down"]


def kernel(**inputs):
    import concourse.bacc as bacc
    from concourse.bass_utils import run_bass_kernel_spmd

    nc = bacc.Bacc("TRN2", target_bir_lowering=False, num_devices=1)
    arrays = {name: np.ascontiguousarray(inputs[name]) for name in _INS}
    arrays["shape_constants"] = shape_constants()
    args = [nc.dram_tensor(name, a.shape, mybir.dt.from_np(a.dtype), kind="ExternalInput").ap()
            for name, a in arrays.items()]
    result = nc.dram_tensor("result", (BATCH, SEQ, DM), F32, kind="ExternalOutput").ap()
    build(nc, *args, result)
    r = run_bass_kernel_spmd(nc, [arrays], core_ids=[0])
    return r.results[0]["result"]
```
